# Optimizing a Trainium2 kernel written in Bass

```python
import numpy as np
import jax
import jax.numpy as jnp

def _softmax(x, axis=-1):
    return jax.nn.softmax(x, axis=axis)

def _gelu(x):
    return jax.nn.gelu(x, approximate=True)

def _silu(x):
    return jax.nn.silu(x)

def _sigmoid(x):
    return jax.nn.sigmoid(x)

def _layernorm(x, axis=-1, eps=1e-05):
    m = jnp.mean(x, axis=axis, keepdims=True)
    v = jnp.var(x, axis=axis, keepdims=True)
    return (x - m) / jnp.sqrt(v + eps)

def _scatter_add(tgt, idx, src, axis=0):
    return tgt.at[idx].add(src)

def _segment_sum(src, seg, n):
    return jax.ops.segment_sum(src, seg, n)
kernel_name = 'mk_adj_resnorm_d2_adj_r2_0560d5'

def setup_inputs(seed: int=0):
    np.random.seed(seed)
    _w = jnp.asarray

    def _rec_inputs():
        import jax
        import jax.numpy as jnp
        _gk = jax.random.key(seed)
        x = -0.0006008 + 1.001 * jax.random.normal(jax.random.fold_in(_gk, 1), (8192, 128), jnp.float32)
        _w = (1.0 + jnp.arange(8192, dtype=jnp.float32)) ** (-0.5)
        _w = _w / _w.mean()
        _pij = jnp.clip(0.00195312 * _w[:, None] * _w[None, :], 0.0, 1.0)
        _a = jax.random.uniform(jax.random.fold_in(_gk, 2), (8192, 8192)) < _pij
        adj = _a.astype(jnp.int32)
        return (x, adj)
    x, adj = _rec_inputs()

    def _L0_gnn_setup():
        import jax, jax.numpy as jnp
        import numpy as np
        N, D_IN, D_OUT = (5000, 128, 128)
        key = jax.random.key(seed)
        k1, k2, k3, k4 = jax.random.split(key, 4)

        def xavier(k, shape, gain=1.414):
            fan_in, fan_out = (shape[0], shape[1])
            bound = gain * np.sqrt(6.0 / (fan_in + fan_out))
            return jax.random.uniform(k, shape, jnp.float32, -bound, bound)
        return {'input': jax.random.normal(k1, (N, D_IN), jnp.float32), 'adj': jax.random.randint(k2, (N, N), 0, 2, jnp.int32), 'M': N, 'W': xavier(k3, (D_IN, D_OUT)), 'b': jnp.zeros((D_OUT,), jnp.float32), 'a': xavier(k4, (D_OUT, 1))}
    _L0_gnn_all = _L0_gnn_setup()
    _L0_gnn_in = {k: v for k, v in _L0_gnn_all.items() if k in ('W', 'b', 'a')}
    del _L0_gnn_all

    def _L1_gnn_setup():
        import jax, jax.numpy as jnp
        import numpy as np
        N = 4096
        D = 128
        NEG_SLOPE = 0.01
        MASK_VAL = -1000000000000.0
        key = jax.random.key(seed)
        k1, k2, k3, k4 = jax.random.split(key, 4)
        x = jax.random.normal(k1, (N, D), dtype=jnp.float32)
        adj = jax.random.randint(k2, (N, N), 0, 2, dtype=jnp.int32)
        W = jax.random.normal(k3, (D, D), dtype=jnp.float32) * (1.0 / np.sqrt(D))
        a = jax.random.normal(k4, (2 * D, 1), dtype=jnp.float32) * (1.0 / np.sqrt(2 * D))
        return {'x': x, 'adj': adj, 'W': W, 'a': a}
    _L1_gnn_all = _L1_gnn_setup()
    _L1_gnn_in = {k: v for k, v in _L1_gnn_all.items() if k in ('W', 'a')}
    del _L1_gnn_all
    return {'x': x, 'adj': adj, 'L0_gnn_W': _L0_gnn_in['W'], 'L0_gnn_b': _L0_gnn_in['b'], 'L0_gnn_a': _L0_gnn_in['a'], 'L1_gnn_W': _L1_gnn_in['W'], 'L1_gnn_a': _L1_gnn_in['a']}

def reference(x, adj, L0_gnn_W, L0_gnn_b, L0_gnn_a, L1_gnn_W, L1_gnn_a):
    import jax
    import jax.numpy as jnp

    def _L0_gnn_ref(input, adj, M, W, b, a):
        import jax, jax.numpy as jnp
        import numpy as np
        N, D_IN, D_OUT = (5000, 128, 128)
        h = jnp.tanh(input @ W + b)
        inp = input @ W
        e = (h @ a)[:, 0]
        valid = jnp.sum(h, axis=1) != 0
        mask = (adj[:M] > 0) & valid[None, :]
        neg = jnp.asarray(-1e+30, h.dtype)
        scores = jnp.where(mask, e[None, :], neg)
        m = jnp.max(scores, axis=1, keepdims=True)
        w = jnp.where(mask, jnp.exp(scores - m), 0.0)
        denom = jnp.sum(w, axis=1, keepdims=True)
        att = w / jnp.maximum(denom, 1e-30)
        return att @ inp

    def _L1_gnn_ref(x, adj, W, a):
        import jax, jax.numpy as jnp
        import numpy as np
        N = 4096
        D = 128
        NEG_SLOPE = 0.01
        MASK_VAL = -1000000000000.0
        h = x @ W
        e_src = h @ a[:D, 0]
        e_dst = h @ a[D:, 0]
        e = e_src[:, None] + e_dst[None, :]
        e = jnp.where(e > 0, e, NEG_SLOPE * e)
        att_logits = jnp.where(adj > 0, e, MASK_VAL)
        attention = jax.nn.softmax(att_logits, axis=1)
        h_prime = attention @ h
        return jax.nn.elu(h_prime)
    x = _layernorm(x + _L0_gnn_ref(x, adj, 8192, L0_gnn_W, L0_gnn_b, L0_gnn_a), axis=-1)
    x = _layernorm(x + _L1_gnn_ref(x, adj, L1_gnn_W, L1_gnn_a), axis=-1)
    return x

_drawn_inputs = setup_inputs


def setup_inputs(seed=0):
    import zlib

    import numpy as np

    out = dict(_drawn_inputs(seed))
    spreads = {'L0_gnn_b': (0.0, 0.311)}
    factors = {}
    for name, (base, spread) in spreads.items():
        noise = np.random.default_rng([zlib.crc32(name.encode()), seed]).standard_normal(out[name].shape)
        drawn = base * np.exp(spread * noise) if base else spread * noise
        out[name] = jnp.asarray(drawn.astype(out[name].dtype))
    for name, factor in factors.items():
        out[name] = (out[name] * factor).astype(out[name].dtype)
    return out
```

```python
from contextlib import ExitStack

import concourse.bass as bass
from concourse import mybir

P = 128
D = 128
BITS = 16
CT = 8
CW = CT * P
DE = D + 1
AHEAD = 4
XBUF = 4
SLOTS = 8
EPS = 1e-5
SLOPE = 0.01
SHIFT = 30.0
TINY = 1e-37
ONE_BITS = 0x4000
EXP_BITS = 0x7F800000
EXP_TOP = 0x7F000000
PART_TOP = 2.0 ** 14

ALU = mybir.AluOpType
ACT = mybir.ActivationFunctionType
F32 = mybir.dt.float32
F16 = mybir.dt.float16
BF16 = mybir.dt.bfloat16
I32 = mybir.dt.int32
U16 = mybir.dt.uint16
AX = mybir.AxisListType


def wait_apart(engine, waits_apart):
    engine.sem_inc(waits_apart, 1)


class Steps:

    def __init__(self, engine, sem, base=0):
        self.engine, self.sem, self.base, self.n = engine, sem, base, 0

    def did(self, instruction):
        instruction.then_inc(self.sem, 1)
        self.n += 1

    def settle(self):
        self.engine.wait_ge(self.sem, self.base + self.n)


def gat_kernel(nc, x, xT, adj_blocks, W0, b0, a0, W1, W1T, a1, es_dram, out):
    N = x.shape[0]
    T = N // P
    CH = N // CW
    G = T // BITS
    Q = N // 512
    TP = T // 2

    x_v = x.rearrange("(t p) d -> p t d", p=P)
    out_v = out.rearrange("(c t p) d -> c p t d", p=P, t=CT)

    with ExitStack() as ctx:
        def sb(name, shape, dt):
            return ctx.enter_context(nc.sbuf_tensor(name, shape, dt))

        def sem(name):
            return ctx.enter_context(nc.semaphore(name))

        psum = ctx.enter_context(nc.psum_tensor("psum", [P, 8, 512], F32))

        rows = sb("rows", [P, T, 2 * DE], F16)
        packed = sb("packed", [P, CH, G, CW], U16)
        xT_sb = packed[:].rearrange("p c g w -> p (c g w)")[:, 0:XBUF * 2 * 512].bitcast(F32).rearrange(
            "p (b n) -> p b n", b=XBUF)
        nodes = sb("nodes", [P, T, D], F32)
        ARENA = max(2 * SLOTS * CW + CW // 2, T * DE + CW + 7 * CW)
        arena = sb("arena", [P, ARENA], I32)
        adj_in = arena[:, 0:2 * SLOTS * CW].rearrange("p (t w) -> p t w", w=CW)
        seam = arena[:, 2 * SLOTS * CW:2 * SLOTS * CW + CW // 2].bitcast(BF16)
        h_ext = arena[:, 0:T * DE].bitcast(F32).rearrange("p (t e) -> p t e", e=DE)
        rows_d = arena[:, 0:T * DE].bitcast(F16).rearrange("p (t e) -> p t e", e=2 * DE)
        o = T * DE
        es_bc = arena[:, o:o + CW].bitcast(F32)
        o += CW
        marks = arena[:, o:o + CW].bitcast(BF16)
        o += CW
        signs = arena[:, o:o + 2 * CW].bitcast(BF16).rearrange("p (b w) -> p b w", w=2 * CW)
        o += 2 * CW
        mask_c = arena[:, o:o + 2 * CW].bitcast(BF16).rearrange("p (b w) -> p b w", w=2 * CW)
        o += 2 * CW
        mask_d = arena[:, o:o + 2 * CW].bitcast(BF16).rearrange("p (b w) -> p b w", w=2 * CW)

        att = sb("att", [P, CT, DE], F32)
        hid = att[:].rearrange("p t e -> p (t e)")[:, 0:2 * 512].rearrange("p (b n) -> p b n", b=2)

        def exp_buf(c):
            return packed[:, c, :, :].rearrange("p g w -> p (g w)")[:, 0:2 * CW].bitcast(F32).rearrange(
                "p (t d) -> p t d", d=D)

        ident = sb("ident", [P, P], F32)
        ident_b = sb("ident_b", [P, P], BF16)
        zeros = sb("zeros", [P, P], BF16)
        ones = sb("ones", [2, 1], F32)
        pack_w = sb("pack_w", [P, 4, P], BF16)
        W0_sb = sb("W0_sb", [P, D], F32)
        b0_sb = sb("b0_sb", [P, 1], F32)
        a0_sb = sb("a0_sb", [P, 2], F32)
        W1_sb = sb("W1_sb", [P, D + 2], F32)
        W1T_sb = sb("W1T_sb", [P, D], F32)
        a1_sb = sb("a1_sb", [P, 2], F32)
        bit_w = sb("bit_w", [P, BITS], F32)
        big = sb("big", [P, 2], F32)
        big_t = sb("big_t", [2, 1], F32)
        big_d = sb("big_d", [2, 2], F32)
        shift = sb("shift", [P, 4], F32)
        wt = sb("wt", [P, 6, T], F32)
        p_w, q_w, mask_w, inv_w, pow_w, bits_w = (wt[:, n, :] for n in range(6))
        B_w, Bp_w, al_w, be_w, w_lo, w_hi = (wt[:, n, :] for n in range(6))
        esed = sb("esed", [P, T, 2], F32)
        es_row = W1T_sb[0:T, :]
        prod = sb("prod", [P, 2, 2, DE], F32)
        hsum = sb("hsum", [P, D], F32)
        hmean = sb("hmean", [P, D], F32)
        den = sb("den", [P, 9], F32)
        rden = sb("rden", [P, 9], F32)
        lone = sb("lone", [P, CT], F32)
        stats = sb("stats", [P, CT, 6], F32)
        mv = sb("mv", [P, CT, 2], F32)
        var = sb("var", [P, CT], F32)
        std = sb("std", [P, CT], F32)
        rstd = sb("rstd", [P, CT], F32)

        acc0 = psum[:, 0:3, 0:3 * DE].rearrange("p b (t e) -> p b t e", e=DE)

        xT_landed = [sem(f"xT_landed{b}") for b in range(XBUF)]
        weights_landed = sem("weights_landed")
        adj_landed = [sem(f"adj_landed{s}") for s in range(SLOTS)]
        x_landed = sem("x_landed")
        consts_ready = sem("consts_ready")
        waits_apart = sem("waits_apart")
        pool_steps = sem("pool_steps")
        vec_consts = sem("vec_consts")
        hidden_ready = sem("hidden_ready")
        tanh_done = sem("tanh_done")
        e_ready = sem("e_ready")
        inp_ready = sem("inp_ready")
        inp_stored = sem("inp_stored")
        vec_pro = sem("vec_pro")
        vec_mid = sem("vec_mid")
        big_ready = sem("big_ready")
        big_turned = sem("big_turned")
        big_diag = sem("big_diag")
        big_everywhere = sem("big_everywhere")
        shift_ready = sem("shift_ready")
        exp_done = sem("exp_done")
        scale_ready = sem("scale_ready")
        hi_ready = sem("hi_ready")
        prod_ready = sem("prod_ready")
        rows_ready = sem("rows_ready")
        masks_ready = sem("masks_ready")
        masks_used = sem("masks_used")
        pack_w_ready = sem("pack_w_ready")
        packs_ready = sem("packs_ready")
        packs_free = sem("packs_free")
        acc_free = sem("acc_free")
        ln_steps = sem("ln_steps")
        var_ready = sem("var_ready")
        std_ready = sem("std_ready")
        x1_ready = sem("x1_ready")
        wa_ready = sem("wa_ready")
        wa_stored = sem("wa_stored")
        x1_staged = sem("x1_staged")
        turned_ready = sem("turned_ready")
        turned_stored = sem("turned_stored")
        h_ready = sem("h_ready")
        h_stored = sem("h_stored")
        h_ones = sem("h_ones")
        es_turned = sem("es_turned")
        es_stored = sem("es_stored")
        es_saved = sem("es_saved")
        es_landed = sem("es_landed")
        signs_ready = sem("signs_ready")
        marks_ready = sem("marks_ready")
        c_ready = sem("c_ready")
        d_ready = sem("d_ready")
        hsum_steps = sem("hsum_steps")
        pairs_used = sem("pairs_used")
        hi_c_ready = sem("hi_c_ready")
        prod_d_ready = sem("prod_d_ready")
        hi_d_ready = sem("hi_d_ready")
        rows_c_ready = sem("rows_c_ready")
        rows1_ready = sem("rows1_ready")
        mean_steps = sem("mean_steps")
        hmean_ready = sem("hmean_ready")
        d_scaled = sem("d_scaled")
        acc1_free = sem("acc1_free")
        out1_steps = sem("out1_steps")
        att_ready = sem("att_ready")
        relu_done = sem("relu_done")
        elu_exp = sem("elu_exp")
        out_ready = sem("out_ready")
        out_stored = sem("out_stored")

        WEIGHT_DMAS = 6
        block = ctx.enter_context(nc.Block())

        @block.sync
        def _(sp):
            def load_xT(q, b):
                sp.dma_start(xT_sb[:, b, :], xT[:, bass.ts(q, 512)]).then_inc(xT_landed[b], 16)

            for b in range(XBUF):
                load_xT(b, b)

            def load_pair(pair, slot):
                sp.dma_start(adj_in[:, 2 * slot:2 * slot + 2, :], adj_blocks[pair]).then_inc(adj_landed[slot], 16)

            if Q > XBUF:
                with sp.Fori(1, Q // XBUF) as r:
                    for b in range(XBUF):
                        sp.wait_ge(inp_ready, (r - 1) * XBUF + b + 1)
                        load_xT(r * XBUF + b, b)
            for slot in range(SLOTS):
                load_pair(slot, slot)

            def load_turn(r):
                for slot in range(SLOTS):
                    sp.wait_ge(masks_used, (r - 1) * BITS + min(2 * slot + 3, BITS) + AHEAD)
                    load_pair(r * SLOTS + slot, slot)

            if G > 1:
                with sp.Fori(1, G) as r:
                    load_turn(r)
            sp.wait_ge(rows_ready, T)
            sp.dma_start(nodes[:], x_v).then_inc(x_landed, 16)
            with sp.Fori(G, CH * G) as r:
                load_turn(r)

            sp.wait_ge(es_stored, 1)
            sp.dma_start(es_dram.rearrange("(t p) -> t p", p=P), es_row[:]).then_inc(es_saved, 16)
            sp.wait_ge(es_saved, 16)
            es_v = es_dram.rearrange("(c w) -> c w", w=CW)

            def load_es(c):
                if not (isinstance(c, int) and c == 0):
                    sp.wait_ge(signs_ready, c * T)
                sp.dma_start(es_bc, es_v[c].partition_broadcast(P)).then_inc(es_landed, 16)

            def store_out(c):
                sp.wait_ge(out_ready, c + 2)
                sp.dma_start(out_v[c], nodes[:, bass.ds(c * CT, CT), :]).then_inc(out_stored, 16)

            load_es(0)
            load_es(1)
            if CH > 2:
                with sp.Fori(2, CH) as c:
                    load_es(c)
                    store_out(c - 2)
            store_out(CH - 2)
            store_out(CH - 1)
            sp.wait_ge(out_stored, 16 * CH)

        @block.tensor
        def _(pe):
            pe.sem_inc(e_ready, 2)
            pe.sem_inc(masks_used, AHEAD)
            pe.sem_inc(h_ready, 2)
            pe.sem_inc(pairs_used, 2)
            pe.wait_ge(weights_landed, 16 * WEIGHT_DMAS)
            pe.wait_ge(consts_ready, 2)

            with pe.Fori(0, Q // XBUF) as r:
                for xb in range(XBUF):
                    q = r * XBUF + xb
                    b = xb % 2
                    pe.wait_ge(xT_landed[xb], (r + 1) * 16)
                    pe.wait_ge(tanh_done, q + 1)
                    nc.tensor.matmul(psum[:, b, :], W0_sb[:], xT_sb[:, xb, :],
                                     start=True, stop=True).then_inc(hidden_ready, 1)
                    pe.wait_ge(inp_stored, q + 1)
                    for n in range(4):
                        last = nc.tensor.matmul(psum[:, 2 + b, n * D:(n + 1) * D], xT_sb[:, xb, n * P:(n + 1) * P],
                                                W0_sb[:], start=True, stop=True, skip_group_check=True)
                    last.then_inc(inp_ready, 1)
                    pe.wait_ge(tanh_done, q + 3)
                    for n in range(4):
                        last = nc.tensor.matmul(psum[:, 4, bass.ds((q * 4 + n) * 2, 2)], hid[:, b, n * P:(n + 1) * P],
                                                a0_sb[:], start=True, stop=True, skip_group_check=True)
                    last.then_inc(e_ready, 1)

            nc.tensor.matmul(psum[:, 7, 0:2], W1T_sb[:], a1_sb[:], start=True, stop=True).then_inc(wa_ready, 1)

            def spread_maxima(n):
                pe.wait_ge(big_ready, n)
                nc.tensor.transpose(psum[0:2, 5, 128:256], big[:], ident[:]).then_inc(big_turned, 1)
                pe.wait_ge(big_diag, n)
                nc.tensor.matmul(psum[:, 6, 0:2], ones[:].to_broadcast([2, P]), big_d[:], start=True, stop=True).then_inc(big_everywhere, 1)

            spread_maxima(1)

            zero_moving = zeros[:, 0:1]
            pe.wait_ge(exp_done, 1)
            pe.wait_ge(scale_ready, 1)
            pe.wait_ge(inp_stored, Q + 2)
            pe.wait_ge(wa_stored, 1)
            with pe.Fori(0, CH) as c:
                pe.wait_ge(acc_free, c + 1)
                for bank in range(3):
                    nc.tensor.matmul(psum[:, bank, 0:3 * DE], zeros[:], zero_moving.to_broadcast([P, 3 * DE]),
                                     start=True, stop=False, skip_group_check=True)
                with pe.Fori(0, G) as g:
                    for k in range(BITS):
                        jt = g * BITS + k
                        mask = seam if k == 0 else adj_in[:, k - 1, 0:CW // 2].bitcast(BF16)
                        pe.wait_ge(masks_ready, (c * G + g) * BITS + k + 2)
                        pe.wait_ge(rows_ready, jt + 1)
                        for i in range(CT):
                            for part in range(2):
                                nc.tensor.matmul(acc0[:, i // 3, i % 3, :], mask[:, i * P:(i + 1) * P],
                                                 rows[:, jt, part * DE:(part + 1) * DE],
                                                 start=False, stop=True, skip_group_check=True)
                        pe.wait_ge(pack_w_ready, (c * G + g) * BITS + k + 1)
                        for b in range(2):
                            if k == 0:
                                pe.wait_ge(packs_free, (c * G + g) * 2 + b + 1)
                            last = nc.tensor.matmul(psum[:, 4 + b, :], pack_w[:, k % AHEAD, :],
                                                    mask[:, b * 512:(b + 1) * 512],
                                                    start=(k == 0), stop=(k == BITS - 1))
                        last.then_inc(masks_used, 1)

            pe.wait_ge(x1_ready, CH)
            pe.wait_ge(packs_free, 2 * CH * G + 2)

            def turn(r, b):
                pe.wait_ge(x1_staged, r + 1)
                pe.wait_ge(turned_stored, r + 1)
                for n in range(2):
                    last = nc.tensor.transpose(psum[:, b, n * P:(n + 1) * P], prod[:, b, n, 0:D], ident[:])
                last.then_inc(turned_ready, 1)

            def project1(r, b):
                pe.wait_ge(turned_stored, r + 3)
                pe.wait_ge(h_stored, r + 1)
                for n in range(2):
                    last = nc.tensor.matmul(psum[:, 2 + b, n * (D + 2):(n + 1) * (D + 2)], hid[:, b, n * P:(n + 1) * P],
                                            W1_sb[:], start=True, stop=True, skip_group_check=True)
                last.then_inc(h_ready, 1)

            turn(0, 0)
            with pe.Fori(0, T // 4 - 1) as r:
                turn(r * 2 + 1, 1)
                project1(r * 2, 0)
                turn(r * 2 + 2, 0)
                project1(r * 2 + 1, 1)
            turn(T // 2 - 1, 1)
            project1(T // 2 - 2, 0)
            project1(T // 2 - 1, 1)

            pe.wait_ge(h_stored, T // 2 + 2)
            nc.tensor.transpose(psum[0:T, 7, 0:P], esed[:, :, 0], ident[:]).then_inc(es_turned, 1)
            spread_maxima(2)

            pe.wait_ge(es_stored, 1)
            pe.wait_ge(scale_ready, 2)
            with pe.Fori(0, CH) as c:
                for i in range(CT):
                    pe.wait_ge(acc1_free, c * CT + i + 1)
                    nc.tensor.matmul(psum[:, i, 0:2 * DE], zeros[:], zero_moving.to_broadcast([P, 2 * DE]),
                                     start=True, stop=False, skip_group_check=True)
                with pe.Fori(0, TP // 2) as r:
                    for b in range(2):
                        m = r * 2 + b
                        pe.wait_ge(d_ready, c * TP + m + 2)
                        for n in range(2):
                            jt = m * 2 + n
                            pe.wait_ge(rows1_ready, jt + 1)
                            for i in range(CT):
                                at = n * CW + i * P
                                for side, mask, source in ((0, mask_c, rows), (1, mask_d, rows_d)):
                                    for part in range(2):
                                        last = nc.tensor.matmul(psum[:, i, side * DE:(side + 1) * DE],
                                                                mask[:, b, at:at + P],
                                                                source[:, jt, part * DE:(part + 1) * DE],
                                                                start=False, stop=True, skip_group_check=True)
                        last.then_inc(pairs_used, 1)

        @block.scalar
        def _(act):
            act.sem_inc(tanh_done, 2)
            act.sem_inc(inp_stored, 2)
            act.sem_inc(packs_free, 2)
            act.sem_inc(turned_stored, 2)
            for dst, src in ((W0_sb[:], W0), (b0_sb[:], b0.rearrange("(d o) -> d o", o=1)), (a0_sb[:, 0:1], a0),
                             (W1_sb[:, 0:D], W1), (W1T_sb[:], W1T), (a1_sb[:], a1)):
                act.dma_start(dst, src).then_inc(weights_landed, 16)
            act.wait_ge(weights_landed, 16 * WEIGHT_DMAS)

            with act.Fori(0, Q // 2) as r:
                for b in range(2):
                    q = r * 2 + b
                    act.wait_ge(hidden_ready, q + 1)
                    act.wait_ge(e_ready, q + 1)
                    nc.scalar.activation(hid[:, b, :], psum[:, b, :], ACT.Tanh, bias=b0_sb[:, 0:1]).then_inc(tanh_done, 1)
                    act.wait_ge(inp_ready, q + 1)
                    wait_apart(act, waits_apart)
                    nc.scalar.activation(nodes[:, bass.ds(q * 4, 4), :].rearrange("p t d -> p (t d)"),
                                         psum[:, 2 + b, :], ACT.Copy).then_inc(inp_stored, 1)

            act.wait_ge(wa_ready, 1)
            nc.scalar.activation(W1_sb[:, D:D + 2], psum[:, 7, 0:2], ACT.Copy).then_inc(wa_stored, 1)

            act.wait_ge(shift_ready, 1)
            nc.scalar.activation(p_w, psum[:, 4, 0:2 * T].rearrange("p (t two) -> p t two", two=2)[:, :, 0], ACT.Exp,
                                 bias=shift[:, 0:1]).then_inc(exp_done, 1)

            act.wait_ge(scale_ready, 1)
            with act.Fori(0, T // 4) as r:
                for n in range(4):
                    nc.scalar.activation(rows[:, r * 4 + n, 0:D], nodes[:, r * 4 + n, :], ACT.Copy,
                                         scale=q_w[:, bass.ds(r * 4 + n, 1)]).then_inc(hi_ready, 1)

            def sqrt_var(n):
                act.wait_ge(var_ready, n)
                nc.scalar.activation(std[:], var[:], ACT.Sqrt).then_inc(std_ready, 1)

            with act.Fori(0, CH) as c:
                with act.Fori(0, G) as g:
                    act.wait_ge(masks_used, (c * G + g + 1) * BITS + AHEAD)
                    wait_apart(act, waits_apart)
                    for b in range(2):
                        nc.scalar.activation(packed[:, c, g, b * 512:(b + 1) * 512], psum[:, 4 + b, :], ACT.Copy,
                                             bias=65535.0, scale=-1.0).then_inc(packs_free, 1)
                sqrt_var(c + 1)

            def stage_x1(q, b):
                nc.scalar.activation(prod[:, b, :, 0:D], nodes[:, bass.ds(q * 2, 2), :], ACT.Copy).then_inc(x1_staged, 1)

            def store_turned(q, b):
                act.wait_ge(turned_ready, q + 1)
                act.wait_ge(h_ready, q + 1)
                nc.scalar.activation(hid[:, b, 0:2 * P], psum[:, b, 0:2 * P], ACT.Copy).then_inc(turned_stored, 1)

            act.wait_ge(x1_ready, CH)
            stage_x1(0, 0)
            with act.Fori(0, T // 4 - 1) as r:
                stage_x1(r * 2 + 1, 1)
                store_turned(r * 2, 0)
                stage_x1(r * 2 + 2, 0)
                store_turned(r * 2 + 1, 1)
            stage_x1(T // 2 - 1, 1)
            store_turned(T // 2 - 2, 0)
            store_turned(T // 2 - 1, 1)

            act.wait_ge(es_turned, 1)
            nc.scalar.activation(es_row[:], psum[0:T, 7, 0:P], ACT.Copy).then_inc(es_stored, 1)

            act.wait_ge(shift_ready, 2)
            nc.scalar.activation(B_w, esed[:, :, 1], ACT.Exp, bias=shift[:, 0:1])
            nc.scalar.activation(Bp_w, esed[:, :, 1], ACT.Exp, bias=shift[:, 1:2], scale=SLOPE)
            nc.scalar.activation(al_w, w_lo, ACT.Exp)
            nc.scalar.activation(be_w, w_hi, ACT.Exp, scale=-1.0).then_inc(exp_done, 1)
            act.wait_ge(scale_ready, 2)

            def hi_parts(jt, b):
                nc.scalar.activation(rows[:, jt, 0:DE], h_ext[:, jt, :], ACT.Copy,
                                     scale=B_w[:, bass.ds(jt, 1)]).then_inc(hi_c_ready, 1)
                act.wait_ge(prod_d_ready, jt + 1)
                act.wait_ge(hi_c_ready, jt + 1)
                wait_apart(act, waits_apart)
                nc.scalar.activation(rows_d[:, jt, 0:DE], prod[:, 1, b, :], ACT.Copy).then_inc(hi_d_ready, 1)

            def sign_turn(c, r, first):
                for k in range(4):
                    jt = r * 4 + k
                    if k % 2 == 0:
                        act.wait_ge(c_ready, c * TP + r * 2 + k // 2 + 1)
                        wait_apart(act, waits_apart)
                    nc.scalar.activation(signs[:, k // 2, (k % 2) * CW:(k % 2 + 1) * CW], es_bc, ACT.Sign,
                                         bias=esed[:, jt, 1:2]).then_inc(signs_ready, 1)
                    if first:
                        hi_parts(jt, k % 2)

            def scale_d(c):
                act.wait_ge(pairs_used, (c + 1) * TP + 2)
                act.wait_ge(out_ready, c + 1)
                wait_apart(act, waits_apart)
                for i in range(CT):
                    nc.scalar.activation(att[:, i, :], psum[:, i, DE:2 * DE], ACT.Copy,
                                         scale=be_w[:, bass.ds(c * CT + i, 1)]).then_inc(d_scaled, 1)

            def elu_and_sqrt(c):
                act.wait_ge(att_ready, c + 1)
                wait_apart(act, waits_apart)
                nc.scalar.activation(exp_buf(c), att[:, :, 0:D], ACT.Relu, scale=-1.0).then_inc(relu_done, 1)
                act.wait_ge(relu_done, c + 1)
                wait_apart(act, waits_apart)
                nc.scalar.activation(exp_buf(c), exp_buf(c), ACT.Exp, scale=-1.0).then_inc(elu_exp, 1)
                sqrt_var(CH + c + 1)

            act.wait_ge(es_landed, 16)
            with act.Fori(0, T // 4) as r:
                sign_turn(0, r, True)
            with act.Fori(1, CH) as c:
                act.wait_ge(es_landed, (c + 1) * 16)
                sign_turn(c, 0, False)
                scale_d(c - 1)
                sign_turn(c, 1, False)
                sign_turn(c, 2, False)
                elu_and_sqrt(c - 1)
                with act.Fori(3, T // 4) as r:
                    sign_turn(c, r, False)
            scale_d(CH - 1)
            elu_and_sqrt(CH - 1)

        @block.vector
        def _(dve):
            dve.sem_inc(acc_free, 1)
            dve.sem_inc(h_stored, 2)
            dve.sem_inc(c_ready, 2)
            dve.sem_inc(acc1_free, CT)
            dve.sem_inc(masks_ready, 1)
            dve.sem_inc(d_ready, 1)
            dve.sem_inc(out_ready, 1)
            consts = Steps(dve, vec_consts)
            consts.did(nc.vector.memset(zeros[:], 0.0))
            consts.did(nc.vector.memset(ones[:], 1.0))
            consts.did(nc.vector.memset(a0_sb[:, 1:2], 1.0))
            consts.did(nc.vector.memset(big[:], 0.0))
            for k in range(BITS):
                consts.did(nc.vector.memset(bit_w[:, k:k + 1], float(2 ** k)))
            consts.settle()
            dve.sem_inc(consts_ready, 1)

            with dve.Fori(0, Q) as q:
                dve.wait_ge(inp_stored, q + 3)
                nc.vector.tensor_reduce(bits_w[:, bass.ds(q * 4, 4)], nodes[:, bass.ds(q * 4, 4), :], AX.X, ALU.max,
                                        apply_absolute_value=True).then_inc(vec_pro, 1)
            pro = Steps(dve, vec_pro, Q)

            def spread_maxima(n):
                dve.wait_ge(big_turned, n)
                pro.did(nc.vector.tensor_reduce(big_t[:], psum[0:2, 5, 128:256], AX.X, ALU.max))
                pro.settle()
                nc.vector.tensor_scalar(big_d[:], ident[0:2, 0:2], big_t[:, 0:1], None, ALU.mult).then_inc(big_diag, 1)
                dve.wait_ge(big_everywhere, n)

            e_all = psum[:, 4, 0:2 * T].rearrange("p (t two) -> p t two", two=2)
            dve.wait_ge(e_ready, Q + 2)
            nc.vector.tensor_reduce(big[:, 0:1], e_all[:, :, 0], AX.X, ALU.max).then_inc(big_ready, 1)
            dve.wait_ge(consts_ready, 2)
            spread_maxima(1)
            nc.vector.tensor_scalar(shift[:, 0:1], psum[:, 6, 0:1], -1.0, SHIFT, ALU.mult, ALU.add).then_inc(shift_ready, 1)
            dve.wait_ge(exp_done, 1)
            pro.did(nc.vector.scalar_tensor_tensor(out=p_w, in0=e_all[:, :, 1], scalar=0.0, in1=p_w,
                                                   op0=ALU.not_equal, op1=ALU.mult))
            pro.settle()
            pro.did(nc.vector.scalar_tensor_tensor(out=bits_w, in0=bits_w, scalar=1.0, in1=p_w,
                                                   op0=ALU.max, op1=ALU.mult))
            pro.settle()
            pro.did(nc.vector.tensor_scalar(bits_w, bits_w, 2.0 ** -100, None, ALU.max))
            pro.settle()
            pro.did(nc.vector.tensor_scalar(mask_w.bitcast(I32), bits_w.bitcast(I32), EXP_BITS, None, ALU.bitwise_and))
            pro.settle()
            pro.did(nc.vector.tensor_scalar(inv_w.bitcast(I32), mask_w.bitcast(I32), -1.0, float(EXP_TOP),
                                            ALU.mult, ALU.add))
            pro.settle()
            pro.did(nc.vector.scalar_tensor_tensor(out=q_w, in0=inv_w, scalar=PART_TOP, in1=p_w,
                                                   op0=ALU.mult, op1=ALU.mult))
            pro.did(nc.vector.tensor_tensor(pow_w.rearrange("p (g k) -> p g k", k=BITS),
                                            inv_w.rearrange("p (g k) -> p g k", k=BITS),
                                            bit_w[:].rearrange("p (o k) -> p o k", o=1).to_broadcast([P, G, BITS]),
                                            ALU.mult))
            pro.settle()
            pro.did(nc.vector.tensor_copy(rows[:, :, D], q_w))
            pro.settle()
            nc.vector.tensor_tensor(rows[:, :, DE + D], q_w, rows[:, :, D], ALU.subtract).then_inc(scale_ready, 1)

            def make_mask(c, g, k):
                n = (c * G + g) * BITS + k
                jt = g * BITS + k
                mask = seam if k == 0 else adj_in[:, k - 1, 0:CW // 2].bitcast(BF16)
                if k % 2 == 0:
                    dve.wait_ge(adj_landed[k // 2], (c * G + g + 1) * 16)
                dve.wait_ge(masks_used, n + 1)
                dve.wait_ge(masks_ready, n + 1)
                nc.vector.tensor_scalar(mask, adj_in[:, k, :], 0.0, mask_w[:, bass.ds(jt, 1)],
                                        ALU.is_gt, ALU.mult).then_inc(masks_ready, 1)
                nc.vector.tensor_scalar(pack_w[:, k % AHEAD, :], ident_b[:], pow_w[:, bass.ds(jt, 1)], None,
                                        ALU.mult).then_inc(pack_w_ready, 1)

            def ln_stats(steps, c):
                steps.settle()
                wait_apart(dve, waits_apart)
                for i in range(CT):
                    steps.did(nc.vector.bn_stats(stats[:, i, :], nodes[:, c * CT + i, :]))
                steps.settle()
                wait_apart(dve, waits_apart)
                for i in range(CT):
                    steps.did(nc.vector.bn_aggr(mv[:, i, :], stats[:, i, :]))
                steps.settle()
                nc.vector.tensor_scalar(var[:], mv[:, :, 1], EPS, None, ALU.add).then_inc(var_ready, 1)

            def ln_apply(steps, c, n):
                dve.wait_ge(std_ready, n)
                steps.did(nc.vector.reciprocal(rstd[:], std[:]))
                steps.settle()
                for i in range(CT):
                    last = nc.vector.tensor_scalar(nodes[:, c * CT + i, :], nodes[:, c * CT + i, :],
                                                   mv[:, i, 0:1], rstd[:, i:i + 1], ALU.subtract, ALU.mult)
                return last

            LN_STEPS = 2 * CT + 1
            with dve.Fori(0, CH) as c:
                with dve.Fori(0, G) as g:
                    for k in range(BITS):
                        make_mask(c, g, k)
                steps = Steps(dve, ln_steps, c * (2 + LN_STEPS))
                dve.wait_ge(masks_used, (c + 1) * T + AHEAD)
                steps.did(nc.vector.tensor_scalar(den[:].rearrange("p (b t) -> p b t", t=3), acc0[:, :, :, D],
                                                  TINY, None, ALU.max))
                steps.settle()
                steps.did(nc.vector.reciprocal(rden[:], den[:]))
                steps.settle()
                dve.wait_ge(x_landed, 16)
                for i in range(CT):
                    last = nc.vector.scalar_tensor_tensor(out=nodes[:, c * CT + i, :], in0=acc0[:, i // 3, i % 3, 0:D],
                                                          scalar=rden[:, i:i + 1], in1=nodes[:, c * CT + i, :],
                                                          op0=ALU.mult, op1=ALU.add)
                last.then_inc(acc_free, 1)
                dve.wait_ge(acc_free, c + 2)
                ln_stats(steps, c)
                ln_apply(steps, c, c + 1).then_inc(x1_ready, 1)
                assert steps.n == 2 + LN_STEPS

            dve.wait_ge(x1_ready, CH)
            mid = Steps(dve, vec_mid)
            mid.did(nc.vector.memset(h_ext[:, :, D], 1.0))
            h_top = w_hi
            with dve.Fori(0, T // 4) as r:
                for b in range(2):
                    q = r * 2 + b
                    pair = psum[:, 2 + b, 0:2 * (D + 2)].rearrange("p (t e) -> p t e", e=D + 2)
                    dve.wait_ge(h_ready, q + 3)
                    nc.vector.tensor_copy(h_ext[:, bass.ds(q * 2, 2), 0:D], pair[:, :, 0:D])
                    nc.vector.tensor_copy(esed[:, bass.ds(q * 2, 2), :], pair[:, :, D:D + 2])
                    nc.vector.tensor_reduce(h_top[:, bass.ds(q, 1)], pair[:, :, 0:D], AX.XY, ALU.max,
                                            apply_absolute_value=True).then_inc(h_stored, 1)
            dve.wait_ge(h_stored, T // 2 + 2)
            mid.did(nc.vector.tensor_reduce(big[:, 0:1], esed[:, :, 1], AX.X, ALU.max))
            nc.vector.tensor_reduce(big[:, 1:2], h_top[:, 0:T // 2], AX.X, ALU.max).then_inc(big_ready, 1)
            pro.base, pro.n = pro.base + pro.n, 0
            spread_maxima(2)
            mid.did(nc.vector.tensor_scalar(shift[:, 0:1], psum[:, 6, 0:1], -1.0, None, ALU.mult))
            mid.did(nc.vector.tensor_scalar(shift[:, 1:2], psum[:, 6, 0:1], -SLOPE, None, ALU.mult))
            mid.settle()
            mid.did(nc.vector.tensor_scalar(mask_w, esed[:, :, 0], shift[:, 0:1], 1.0 - SLOPE, ALU.subtract, ALU.mult))
            mid.settle()
            mid.did(nc.vector.tensor_scalar(w_lo, mask_w, 0.0, None, ALU.min))
            nc.vector.tensor_scalar(w_hi, mask_w, 0.0, None, ALU.max).then_inc(shift_ready, 1)
            mid.did(nc.vector.tensor_scalar(shift[:, 2:3], psum[:, 6, 1:2], 1.0, None, ALU.max))
            mid.settle()
            mid.did(nc.vector.tensor_scalar(shift[:, 2:3].bitcast(I32), shift[:, 2:3].bitcast(I32), EXP_BITS, None,
                                            ALU.bitwise_and))
            mid.settle()
            mid.did(nc.vector.tensor_scalar(shift[:, 2:3].bitcast(I32), shift[:, 2:3].bitcast(I32), -1.0,
                                            float(EXP_TOP), ALU.mult, ALU.add))
            mid.settle()
            dve.wait_ge(exp_done, 2)
            mid.did(nc.vector.tensor_scalar(B_w, B_w, shift[:, 2:3], PART_TOP, ALU.mult, ALU.mult))
            nc.vector.tensor_scalar(Bp_w, Bp_w, shift[:, 2:3], PART_TOP, ALU.mult, ALU.mult).then_inc(scale_ready, 1)

            def make_pair(c, g, kk):
                m = (c * G + g) * (BITS // 2) + kk
                b = kk % 2
                dve.wait_ge(d_ready, m + 1)
                for n in range(2):
                    bit = 2 * kk + n
                    by, way = (14 - bit, ALU.logical_shift_left) if bit <= 14 else (bit - 14, ALU.logical_shift_right)
                    last = nc.vector.tensor_scalar(marks[:, n * CW:(n + 1) * CW].bitcast(U16), packed[:, c, g, :],
                                                   by, ONE_BITS, way, ALU.bitwise_and)
                last.then_inc(marks_ready, 1)
                dve.wait_ge(marks_ready, m + 1)
                dve.wait_ge(signs_ready, 2 * m + 2)
                dve.wait_ge(pairs_used, m + 1)
                nc.vector.tensor_tensor(mask_c[:, b, :], signs[:, b, :], marks, ALU.is_gt).then_inc(c_ready, 1)
                dve.wait_ge(c_ready, m + 3)
                nc.vector.tensor_tensor(mask_d[:, b, :], mask_c[:, b, :], marks, ALU.is_equal).then_inc(d_ready, 1)

            def add_c(steps, c):
                for i in range(CT):
                    dve.wait_ge(d_scaled, c * CT + i + 1)
                    nc.vector.scalar_tensor_tensor(out=att[:, i, :], in0=psum[:, i, 0:DE],
                                                   scalar=al_w[:, bass.ds(c * CT + i, 1)], in1=att[:, i, :],
                                                   op0=ALU.mult, op1=ALU.add).then_inc(acc1_free, 1)
                dve.wait_ge(acc1_free, (c + 2) * CT)

            def divide(steps, c):
                steps.did(nc.vector.tensor_scalar(lone[:], att[:, :, D], 0.0, None, ALU.is_le))
                steps.did(nc.vector.tensor_scalar(den[:, 0:CT], att[:, :, D], TINY, None, ALU.max))
                steps.settle()
                steps.did(nc.vector.reciprocal(rden[:, 0:CT], den[:, 0:CT]))
                steps.settle()
                for i in range(CT):
                    steps.did(nc.vector.tensor_scalar(att[:, i, 0:D], att[:, i, 0:D], rden[:, i:i + 1], None, ALU.mult))
                steps.settle()
                dve.wait_ge(hmean_ready, 1)
                for i in range(CT):
                    last = nc.vector.scalar_tensor_tensor(out=att[:, i, 0:D], in0=hmean[:], scalar=lone[:, i:i + 1],
                                                          in1=att[:, i, 0:D], op0=ALU.mult, op1=ALU.add)
                last.then_inc(att_ready, 1)

            def add_elu(steps, c):
                dve.wait_ge(elu_exp, c + 1)
                dve.wait_ge(att_ready, c + 1)
                steps.did(nc.vector.scalar_tensor_tensor(out=exp_buf(c), in0=att[:, :, 0:D], scalar=0.0, in1=exp_buf(c),
                                                         op0=ALU.max, op1=ALU.add))
                steps.settle()
                x1 = nodes[:, bass.ds(c * CT, CT), :]
                steps.did(nc.vector.scalar_tensor_tensor(out=x1, in0=exp_buf(c), scalar=-1.0, in1=x1,
                                                         op0=ALU.add, op1=ALU.add))
                ln_stats(steps, c)

            def finish(steps, c):
                ln_apply(steps, c, CH + c + 1).then_inc(out_ready, 1)

            OUT_STEPS = 3 + CT + 2 + LN_STEPS
            for kk in range(BITS // 2):
                make_pair(0, 0, kk)
            if G > 1:
                with dve.Fori(1, G) as g:
                    for kk in range(BITS // 2):
                        make_pair(0, g, kk)
            with dve.Fori(1, CH) as c:
                steps = Steps(dve, out1_steps, (c - 1) * OUT_STEPS)
                pieces = {0: add_c, 2: divide, 3: add_elu, 4: finish}
                for kk in range(BITS // 2):
                    make_pair(c, 0, kk)
                    if kk in pieces:
                        pieces[kk](steps, c - 1)
                assert steps.n == OUT_STEPS
                if G > 1:
                    with dve.Fori(1, G) as g:
                        for kk in range(BITS // 2):
                            make_pair(c, g, kk)
            steps = Steps(dve, out1_steps, (CH - 1) * OUT_STEPS)
            for piece in (add_c, divide, add_elu, finish):
                piece(steps, CH - 1)

        @block.gpsimd
        def _(pool):
            own = Steps(pool, pool_steps)
            own.did(nc.gpsimd.memset(ident[:], 0.0))
            own.settle()
            own.did(nc.gpsimd.affine_select(out=ident[:], in_=ident[:], compare_op=ALU.not_equal, fill=1.0,
                                            base=0, pattern=[[-1, P]], channel_multiplier=1))
            own.settle()
            nc.gpsimd.tensor_copy(ident_b[:], ident[:]).then_inc(consts_ready, 1)

            pool.wait_ge(scale_ready, 1)
            with pool.Fori(0, T // 2) as r:
                for b in range(2):
                    jt = r * 2 + b
                    nc.gpsimd.tensor_tensor(prod[:, 0, b, 0:D], nodes[:, jt, :],
                                            q_w[:, bass.ds(jt, 1)].to_broadcast([P, D]), ALU.mult).then_inc(prod_ready, 1)
                    pool.wait_ge(prod_ready, jt + 1)
                    pool.wait_ge(hi_ready, jt + 1)
                    wait_apart(pool, waits_apart)
                    nc.gpsimd.tensor_tensor(rows[:, jt, DE:DE + D], prod[:, 0, b, 0:D], rows[:, jt, 0:D],
                                            ALU.subtract).then_inc(rows_ready, 1)
                    pool.wait_ge(rows_ready, jt + 1)
                    wait_apart(pool, waits_apart)

            nc.gpsimd.memset(hsum[:], 0.0).then_inc(hsum_steps, 1)
            with pool.Fori(0, T // 2) as r:
                pool.wait_ge(h_stored, r + 3)
                for b in range(2):
                    pool.wait_ge(hsum_steps, r * 2 + b + 1)
                    wait_apart(pool, waits_apart)
                    nc.gpsimd.tensor_tensor(hsum[:], hsum[:], h_ext[:, r * 2 + b, 0:D], ALU.add).then_inc(hsum_steps, 1)

            pool.wait_ge(hsum_steps, T + 1)
            pool.wait_ge(scale_ready, 2)
            with pool.Fori(0, T // 2) as r:
                for b in range(2):
                    jt = r * 2 + b
                    nc.gpsimd.tensor_tensor(prod[:, 0, b, :], h_ext[:, jt, :],
                                            B_w[:, bass.ds(jt, 1)].to_broadcast([P, DE]), ALU.mult).then_inc(prod_ready, 1)
                    nc.gpsimd.tensor_tensor(prod[:, 1, b, :], h_ext[:, jt, :],
                                            Bp_w[:, bass.ds(jt, 1)].to_broadcast([P, DE]), ALU.mult).then_inc(prod_d_ready, 1)
                    pool.wait_ge(prod_ready, T + jt + 1)
                    pool.wait_ge(hi_c_ready, jt + 1)
                    wait_apart(pool, waits_apart)
                    nc.gpsimd.tensor_tensor(rows[:, jt, DE:2 * DE], prod[:, 0, b, :], rows[:, jt, 0:DE],
                                            ALU.subtract).then_inc(rows_c_ready, 1)
                    pool.wait_ge(prod_d_ready, jt + 1)
                    pool.wait_ge(hi_d_ready, jt + 1)
                    wait_apart(pool, waits_apart)
                    nc.gpsimd.tensor_tensor(rows_d[:, jt, DE:2 * DE], prod[:, 1, b, :], rows_d[:, jt, 0:DE],
                                            ALU.subtract).then_inc(rows1_ready, 1)
                    pool.wait_ge(rows_c_ready, jt + 1)
                    pool.wait_ge(rows1_ready, jt + 1)
                    wait_apart(pool, waits_apart)

            nc.gpsimd.partition_all_reduce(hmean[:], hsum[:], P, bass.bass_isa.ReduceOp.add).then_inc(mean_steps, 1)
            pool.wait_ge(mean_steps, 1)
            nc.gpsimd.tensor_scalar(hmean[:], hmean[:], 1.0 / N, 1.0, ALU.mult, ALU.mult).then_inc(hmean_ready, 1)


def kernel(x, adj, L0_gnn_W, L0_gnn_b, L0_gnn_a, L1_gnn_W, L1_gnn_a):
    import numpy as np
    import concourse.bacc as bacc
    from concourse.bass_utils import run_bass_kernel_spmd

    x, adj, W1 = np.asarray(x), np.asarray(adj), np.asarray(L1_gnn_W)
    N = x.shape[0]
    blocks = adj.reshape(N // CW, CW, N // (2 * P), 2, P).transpose(0, 2, 4, 3, 1)
    arrays = {
        "x": x, "xT": x.T, "adj_blocks": blocks.reshape(-1, P, 2, CW),
        "W0": np.asarray(L0_gnn_W), "b0": np.asarray(L0_gnn_b), "a0": np.asarray(L0_gnn_a),
        "W1": W1, "W1T": W1.T, "a1": np.asarray(L1_gnn_a).reshape(2, D).T,
    }
    arrays = {name: np.ascontiguousarray(a) for name, a in arrays.items()}

    nc = bacc.Bacc("TRN2", target_bir_lowering=False, num_devices=1)
    aps = [nc.dram_tensor(name, a.shape, mybir.dt.from_np(a.dtype), kind="ExternalInput").ap()
           for name, a in arrays.items()]
    es_dram = nc.dram_tensor("es_by_node", (N,), F32, kind="Internal").ap()
    out = nc.dram_tensor("out", (N, D), F32, kind="ExternalOutput").ap()
    gat_kernel(nc, *aps, es_dram, out)
    return run_bass_kernel_spmd(nc, [arrays], core_ids=[0]).results[0]["out"]
```

```python
from contextlib import ExitStack

import concourse.bass as bass
from concourse import mybir

P = 128
D = 128
BITS = 16
CT = 8
CW = CT * P
DE = D + 1
AHEAD = 4
XBUF = 4
SLOTS = 8
HALF = CT // 2
BUFS = 4
EPS = 1e-5
SLOPE = 0.01
SHIFT = 30.0
TINY = 1e-37
ONE_BITS = 0x4000
EXP_BITS = 0x7F800000
EXP_TOP = 0x7F000000
PART_TOP = 2.0 ** 14

ALU = mybir.AluOpType
ACT = mybir.ActivationFunctionType
F32 = mybir.dt.float32
F16 = mybir.dt.float16
BF16 = mybir.dt.bfloat16
I32 = mybir.dt.int32
U16 = mybir.dt.uint16
AX = mybir.AxisListType


def wait_apart(engine, waits_apart):
    engine.sem_inc(waits_apart, 1)


class Steps:

    def __init__(self, engine, sem, base=0):
        self.engine, self.sem, self.base, self.n = engine, sem, base, 0

    def did(self, instruction):
        instruction.then_inc(self.sem, 1)
        self.n += 1

    def settle(self):
        self.engine.wait_ge(self.sem, self.base + self.n)


def gat_kernel(nc, x, xT, adj_blocks, W0, b0, a0, W1, W1T, a1, es_dram, x1_dram, out):
    N = x.shape[0]
    T = N // P
    CH = N // CW
    G = T // BITS
    Q = N // 512
    TP = T // 2
    QC = CT // 2
    assert G >= 2 and Q % XBUF == 0

    x_v = x.rearrange("(t p) d -> p t d", p=P)
    out_v = out.rearrange("(c t p) d -> c p t d", p=P, t=CT)
    x1_v = x1_dram.rearrange("(c t p) d -> c p t d", p=P, t=CT)
    es_v = es_dram.rearrange("(c w) -> c w", w=CW)

    with ExitStack() as ctx:
        def sb(name, shape, dt):
            return ctx.enter_context(nc.sbuf_tensor(name, shape, dt))

        def sem(name):
            return ctx.enter_context(nc.semaphore(name))

        psum = ctx.enter_context(nc.psum_tensor("psum", [P, 8, 512], F32))

        rows = sb("rows", [P, T, 2 * DE], F16)
        packed = sb("packed", [P, CH, max(G, 4), CW], U16)
        xT_sb = packed[:].rearrange("p c g w -> p (c g w)")[:, 0:XBUF * 2 * 512].bitcast(F32).rearrange(
            "p (b n) -> p b n", b=XBUF)
        nodes_ext = sb("nodes", [P, T, DE], F32)
        nodes = nodes_ext[:, :, 0:D]
        rows_d = nodes_ext[:].rearrange("p t e -> p (t e)").bitcast(F16).rearrange("p (t e) -> p t e", e=2 * DE)
        arena = sb("arena", [P, 2 * SLOTS * CW + CW // 2], I32)
        adj_in = arena[:, 0:2 * SLOTS * CW].rearrange("p (t w) -> p t w", w=CW)
        seam = arena[:, 2 * SLOTS * CW:2 * SLOTS * CW + CW // 2].bitcast(BF16)
        es_bc = arena[:, 0:2 * CW].bitcast(F32)
        marks = arena[:, 2 * CW:3 * CW].bitcast(BF16)
        signs, mask_c, mask_d = (
            arena[:, (3 + n * BUFS) * CW:(3 + (n + 1) * BUFS) * CW].bitcast(BF16).rearrange("p (b w) -> p b w", w=2 * CW)
            for n in range(3))

        att = sb("att", [P, CT, DE], F32)
        hid = att[:].rearrange("p t e -> p (t e)")[:, 0:2 * 512].rearrange("p (b n) -> p b n", b=2)

        def over_packed(c, n):
            return packed[:, c, :, :].rearrange("p g w -> p (g w)")[:, n * 2 * CW:(n + 1) * 2 * CW].bitcast(F32).rearrange(
                "p (t d) -> p t d", d=D)

        def exp_buf(c):
            return over_packed(c, 0)

        def x1_buf(c):
            return over_packed(c, 1)

        ident = sb("ident", [P, P], F32)
        ident_b = sb("ident_b", [P, P], BF16)
        zeros = sb("zeros", [P, P], BF16)
        ones = sb("ones", [2, 1], F32)
        pack_w = sb("pack_w", [P, 4, P], BF16)
        W0_sb = sb("W0_sb", [P, D], F32)
        b0_sb = sb("b0_sb", [P, 1], F32)
        a0_sb = sb("a0_sb", [P, 2], F32)
        W1_sb = sb("W1_sb", [P, D + 2], F32)
        W1T_sb = sb("W1T_sb", [P, D], F32)
        a1_sb = sb("a1_sb", [P, 2], F32)
        bit_w = sb("bit_w", [P, BITS], F32)
        big = sb("big", [P, 2], F32)
        big_t = sb("big_t", [2, 1], F32)
        big_d = sb("big_d", [2, 2], F32)
        shift = sb("shift", [P, 4], F32)
        wt = sb("wt", [P, 6, T], F32)
        p_w, q_w, mask_w, inv_w, pow_w, bits_w = (wt[:, n, :] for n in range(6))
        B_w, Bp_w, al_w, be_w, w_lo, w_hi = (wt[:, n, :] for n in range(6))
        esed = sb("esed", [P, T, 2], F32)
        es_row = W1T_sb[0:CT, :]
        es_col = sb("es_col", [P, CT], F32)
        prod = sb("prod", [P, 2, 2, DE], F32)
        hsum = sb("hsum", [P, D], F32)
        hmean = W1T_sb[:]
        h_top = sb("h_top", [P, CH], F32)
        den = sb("den", [P, 9], F32)
        rden = sb("rden", [P, 9], F32)
        lone = sb("lone", [P, CT], F32)
        stats = sb("stats", [P, CT, 6], F32)
        mv = sb("mv", [P, CT, 2], F32)
        var = sb("var", [P, CT], F32)
        std = sb("std", [P, CT], F32)
        rstd = sb("rstd", [P, CT], F32)

        banks = psum[:].rearrange("p b n -> p (b n)")

        def bank(first, n, at, width):
            return banks[:, bass.ds(first * 512 + (n * 512 + at), width)]

        def parity(c):
            return c % 2 if isinstance(c, int) else c & 1

        def acc_bank(c):
            return parity(c) * 3

        xT_landed = [sem(f"xT_landed{b}") for b in range(XBUF)]
        weights_landed = sem("weights_landed")
        adj_landed = [sem(f"adj_landed{s}") for s in range(SLOTS)]
        x_landed = sem("x_landed")
        consts_ready = sem("consts_ready")
        waits_apart = sem("waits_apart")
        pool_steps = sem("pool_steps")
        vec_consts = sem("vec_consts")
        hidden_ready = sem("hidden_ready")
        tanh_done = sem("tanh_done")
        e_ready = sem("e_ready")
        inp_ready = sem("inp_ready")
        inp_stored = sem("inp_stored")
        vec_pro = sem("vec_pro")
        vec_mid = sem("vec_mid")
        big_ready = sem("big_ready")
        big_turned = sem("big_turned")
        big_diag = sem("big_diag")
        big_everywhere = sem("big_everywhere")
        shift_ready = sem("shift_ready")
        exp_done = sem("exp_done")
        scale_ready = sem("scale_ready")
        hi_ready = sem("hi_ready")
        prod_ready = sem("prod_ready")
        rows_ready = sem("rows_ready")
        masks_ready = sem("masks_ready")
        masks_used = sem("masks_used")
        pack_w_ready = sem("pack_w_ready")
        packs_ready = sem("packs_ready")
        packs_free = sem("packs_free")
        ln_steps = sem("ln_steps")
        var_ready = sem("var_ready")
        std_ready = sem("std_ready")
        x1_ready = sem("x1_ready")
        wa_ready = sem("wa_ready")
        wa_stored = sem("wa_stored")
        x1_staged = sem("x1_staged")
        turned_ready = sem("turned_ready")
        turned_stored = sem("turned_stored")
        h_ready = sem("h_ready")
        h_stored = sem("h_stored")
        h_ones = sem("h_ones")
        es_turned = sem("es_turned")
        es_stored = sem("es_stored")
        es_staged = sem("es_staged")
        es_saved = sem("es_saved")
        x1_saved = sem("x1_saved")
        x1_landed = sem("x1_landed")
        h_topped = sem("h_topped")
        es_landed = sem("es_landed")
        signs_ready = sem("signs_ready")
        marks_ready = sem("marks_ready")
        c_ready = sem("c_ready")
        d_ready = sem("d_ready")
        hsum_steps = sem("hsum_steps")
        pairs_used = sem("pairs_used")
        hi_c_ready = sem("hi_c_ready")
        sums_ready = sem("sums_ready")
        norm_done = sem("norm_done")
        prod_d_ready = sem("prod_d_ready")
        hi_d_ready = sem("hi_d_ready")
        rows_c_ready = sem("rows_c_ready")
        rows1_ready = sem("rows1_ready")
        mean_steps = sem("mean_steps")
        hmean_ready = sem("hmean_ready")
        d_scaled = sem("d_scaled")
        acc1_free = sem("acc1_free")
        out1_steps = sem("out1_steps")
        att_ready = sem("att_ready")
        relu_done = sem("relu_done")
        elu_exp = sem("elu_exp")
        out_ready = sem("out_ready")
        out_stored = sem("out_stored")

        WEIGHT_DMAS = 6
        block = ctx.enter_context(nc.Block())

        @block.sync
        def _(sp):
            def load_xT(q, b):
                sp.dma_start(xT_sb[:, b, :], xT[:, bass.ts(q, 512)]).then_inc(xT_landed[b], 16)

            for b in range(XBUF):
                load_xT(b, b)

            def load_pair(pair, slot):
                sp.dma_start(adj_in[:, 2 * slot:2 * slot + 2, :], adj_blocks[pair]).then_inc(adj_landed[slot], 16)

            slots = list(range(SLOTS))
            for r in range(1, Q // XBUF):
                for b in range(XBUF):
                    sp.wait_ge(inp_ready, (r - 1) * XBUF + b + 1)
                    load_xT(r * XBUF + b, b)
                for _ in range(SLOTS // XBUF):
                    load_pair(slots[0], slots.pop(0))
            for slot in slots:
                load_pair(slot, slot)

            def load_turn(r):
                for slot in range(SLOTS):
                    sp.wait_ge(masks_used, (r - 1) * BITS + min(2 * slot + 3, BITS) + AHEAD)
                    load_pair(r * SLOTS + slot, slot)

            with sp.Fori(1, G) as r:
                load_turn(r)
            sp.wait_ge(rows_ready, T)
            sp.dma_start(nodes, x_v).then_inc(x_landed, 16)
            with sp.Fori(G, CH * G) as r:
                load_turn(r)

            def load_es(c):
                if not isinstance(c, int):
                    sp.wait_ge(signs_ready, (c - 1) * T)
                if not (isinstance(c, int) and c == 0):
                    sp.wait_ge(es_landed, c * 16)
                    wait_apart(sp, waits_apart)
                sp.dma_start(es_bc[:, bass.ds(parity(c) * CW, CW)], es_v[c].partition_broadcast(P)).then_inc(es_landed, 16)

            def load_x1(c):
                sp.wait_ge(marks_ready, (c + 1) * TP)
                sp.dma_start(x1_buf(c), x1_v[c]).then_inc(x1_landed, 16)

            def store_out(c):
                sp.wait_ge(out_ready, c + 2)
                sp.dma_start(out_v[c], x1_buf(c)).then_inc(out_stored, 16)

            sp.wait_ge(masks_used, CH * T + AHEAD)
            sp.wait_ge(es_saved, 16 * (CH + 1))
            sp.wait_ge(x1_saved, 16 * CH)
            load_es(0)
            load_es(1)
            if CH > 2:
                with sp.Fori(1, CH - 1) as c:
                    load_x1(c - 1)
                    load_es(c + 1)
                    store_out(c - 1)
            load_x1(CH - 2)
            store_out(CH - 2)
            load_x1(CH - 1)
            store_out(CH - 1)
            sp.wait_ge(out_stored, 16 * CH)

        @block.tensor
        def _(pe):
            pe.sem_inc(e_ready, 2)
            pe.sem_inc(masks_used, AHEAD)
            pe.sem_inc(pairs_used, BUFS)
            pe.wait_ge(weights_landed, 16 * WEIGHT_DMAS)
            pe.wait_ge(consts_ready, 2)

            with pe.Fori(0, Q // XBUF) as r:
                for xb in range(XBUF):
                    q = r * XBUF + xb
                    b = xb % 2
                    pe.wait_ge(xT_landed[xb], (r + 1) * 16)
                    pe.wait_ge(tanh_done, q + 1)
                    nc.tensor.matmul(psum[:, b, :], W0_sb[:], xT_sb[:, xb, :],
                                     start=True, stop=True).then_inc(hidden_ready, 1)
                    pe.wait_ge(inp_stored, q + 1)
                    for n in range(4):
                        last = nc.tensor.matmul(psum[:, 2 + b, n * D:(n + 1) * D], xT_sb[:, xb, n * P:(n + 1) * P],
                                                W0_sb[:], start=True, stop=True, skip_group_check=True)
                    last.then_inc(inp_ready, 1)
                    pe.wait_ge(tanh_done, q + 3)
                    for n in range(4):
                        last = nc.tensor.matmul(psum[:, 4, bass.ds((q * 4 + n) * 2, 2)], hid[:, b, n * P:(n + 1) * P],
                                                a0_sb[:], start=True, stop=True, skip_group_check=True)
                    last.then_inc(e_ready, 1)

            nc.tensor.matmul(psum[:, 7, 0:2], W1T_sb[:], a1_sb[:], start=True, stop=True).then_inc(wa_ready, 1)

            def spread_maxima(n):
                pe.wait_ge(big_ready, n)
                nc.tensor.transpose(psum[0:2, 5, 128:256], big[:], ident[:]).then_inc(big_turned, 1)
                pe.wait_ge(big_diag, n)
                nc.tensor.matmul(psum[:, 6, 0:2], ones[:].to_broadcast([2, P]), big_d[:], start=True, stop=True).then_inc(big_everywhere, 1)

            spread_maxima(1)

            zero_moving = zeros[:, 0:1]
            pe.wait_ge(exp_done, 1)
            pe.wait_ge(scale_ready, 1)
            pe.wait_ge(inp_stored, Q + 2)
            pe.wait_ge(wa_stored, 1)

            def open_sums(c):
                for n in range(3):
                    nc.tensor.matmul(bank(acc_bank(c), n, 0, 3 * DE), zeros[:], zero_moving.to_broadcast([P, 3 * DE]),
                                     start=True, stop=False, skip_group_check=True)

            def add_tiles(c, g, between={}):
                for k in range(BITS):
                    jt = g * BITS + k
                    mask = seam if k == 0 else adj_in[:, k - 1, 0:CW // 2].bitcast(BF16)
                    pe.wait_ge(masks_ready, (c * G + g) * BITS + k + 2)
                    pe.wait_ge(rows_ready, jt + 1)
                    for i in range(CT):
                        for part in range(2):
                            nc.tensor.matmul(bank(acc_bank(c), i // 3, (i % 3) * DE, DE), mask[:, i * P:(i + 1) * P],
                                             rows[:, jt, part * DE:(part + 1) * DE],
                                             start=False, stop=True, skip_group_check=True)
                    pe.wait_ge(pack_w_ready, (c * G + g) * BITS + k + 1)
                    for b in range(2):
                        if k == 0:
                            pe.wait_ge(packs_free, (c * G + g) * 2 + b + 1)
                        last = nc.tensor.matmul(psum[:, 6 + b, :], pack_w[:, k % AHEAD, :],
                                                mask[:, b * 512:(b + 1) * 512],
                                                start=(k == 0), stop=(k == BITS - 1))
                    last.then_inc(masks_used, 1)
                    for step, n in between.get(k, ()):
                        step(c - 1, n)

            def turn(c, n):
                pe.wait_ge(x1_staged, c * QC + n + 1)
                pe.wait_ge(turned_stored, c * QC + n + 1)
                wait_apart(pe, waits_apart)
                for t in range(2):
                    last = nc.tensor.matmul(bank(acc_bank(c), 0, t * P, P), prod[:, n % 2, t, 0:D], ident[:],
                                            start=True, stop=True, skip_group_check=True)
                last.then_inc(turned_ready, 1)

            def project(c, n):
                pe.wait_ge(turned_stored, c * QC + n + 2)
                if n >= 2:
                    pe.wait_ge(h_stored, c * QC + n - 1)
                for t in range(2):
                    last = nc.tensor.matmul(bank(acc_bank(c), 1 + n % 2, t * (D + 2), D + 2),
                                            hid[:, n % 2, t * P:(t + 1) * P], W1_sb[:],
                                            start=True, stop=True, skip_group_check=True)
                last.then_inc(h_ready, 1)

            def turn_es(c, n):
                pe.wait_ge(es_staged, c + 1)
                wait_apart(pe, waits_apart)
                nc.tensor.matmul(bank(acc_bank(c), 0, 0, P)[0:CT, :], es_col[:], ident[:], start=True, stop=True,
                                 skip_group_check=True).then_inc(es_turned, 1)

            open_sums(0)
            with pe.Fori(0, G) as g:
                add_tiles(0, g)
            with pe.Fori(1, CH) as c:
                pe.wait_ge(es_stored, c)
                open_sums(c)
                with pe.Fori(0, G - 1) as g:
                    add_tiles(c, g)
                add_tiles(c, G - 1, {0: [(turn, 0)], 2: [(turn, 1)], 3: [(project, 0)], 5: [(turn, 2)],
                                     6: [(project, 1)], 8: [(turn, 3)], 9: [(project, 2)], 11: [(project, 3)],
                                     13: [(turn_es, 0)]})
            for step, n in ((turn, 0), (turn, 1), (project, 0), (turn, 2), (project, 1), (turn, 3), (project, 2),
                            (project, 3), (turn_es, 0)):
                step(CH - 1, n)

            spread_maxima(2)

            pe.wait_ge(packs_free, 2 * CH * G + 2)
            pe.wait_ge(es_stored, CH + 1)
            pe.wait_ge(scale_ready, 2)
            with pe.Fori(0, CH) as c:
                for i in range(CT):
                    pe.wait_ge(acc1_free, c * CT + i + 1)
                    nc.tensor.matmul(psum[:, i, 0:2 * DE], zeros[:], zero_moving.to_broadcast([P, 2 * DE]),
                                     start=True, stop=False, skip_group_check=True)
                with pe.Fori(0, TP // BUFS) as r:
                    for b in range(BUFS):
                        m = r * BUFS + b
                        pe.wait_ge(d_ready, c * TP + m + 2)
                        for n in range(2):
                            jt = m * 2 + n
                            pe.wait_ge(rows1_ready, jt + 1)
                            for i in range(CT):
                                at = n * CW + i * P
                                for side, mask, source in ((0, mask_c, rows), (1, mask_d, rows_d)):
                                    for part in range(2):
                                        last = nc.tensor.matmul(psum[:, i, side * DE:(side + 1) * DE],
                                                                mask[:, b, at:at + P],
                                                                source[:, jt, part * DE:(part + 1) * DE],
                                                                start=False, stop=True, skip_group_check=True)
                        last.then_inc(pairs_used, 1)

        @block.scalar
        def _(act):
            act.sem_inc(tanh_done, 2)
            act.sem_inc(inp_stored, 2)
            act.sem_inc(packs_free, 2)
            act.sem_inc(turned_stored, 1)
            act.sem_inc(es_stored, 1)
            act.sem_inc(es_saved, 16)
            for dst, src in ((W0_sb[:], W0), (b0_sb[:], b0.rearrange("(d o) -> d o", o=1)), (a0_sb[:, 0:1], a0),
                             (W1_sb[:, 0:D], W1), (W1T_sb[:], W1T), (a1_sb[:], a1)):
                act.dma_start(dst, src).then_inc(weights_landed, 16)
            act.wait_ge(weights_landed, 16 * WEIGHT_DMAS)

            with act.Fori(0, Q // 2) as r:
                for b in range(2):
                    q = r * 2 + b
                    act.wait_ge(hidden_ready, q + 1)
                    act.wait_ge(e_ready, q + 1)
                    nc.scalar.activation(hid[:, b, :], psum[:, b, :], ACT.Tanh, bias=b0_sb[:, 0:1]).then_inc(tanh_done, 1)
                    act.wait_ge(inp_ready, q + 1)
                    wait_apart(act, waits_apart)
                    nc.scalar.activation(nodes[:, bass.ds(q * 4, 4), :],
                                         psum[:, 2 + b, :].rearrange("p (t d) -> p t d", d=D), ACT.Copy).then_inc(inp_stored, 1)

            act.wait_ge(wa_ready, 1)
            nc.scalar.activation(W1_sb[:, D:D + 2], psum[:, 7, 0:2], ACT.Copy).then_inc(wa_stored, 1)

            act.wait_ge(shift_ready, 1)
            nc.scalar.activation(p_w, psum[:, 4, 0:2 * T].rearrange("p (t two) -> p t two", two=2)[:, :, 0], ACT.Exp,
                                 bias=shift[:, 0:1]).then_inc(exp_done, 1)

            act.wait_ge(scale_ready, 1)
            with act.Fori(0, T // 4) as r:
                for n in range(4):
                    nc.scalar.activation(rows[:, r * 4 + n, 0:D], nodes[:, r * 4 + n, :], ACT.Copy,
                                         scale=q_w[:, bass.ds(r * 4 + n, 1)]).then_inc(hi_ready, 1)

            def take_packs(c, g):
                act.wait_ge(masks_used, (c * G + g + 1) * BITS + AHEAD)
                wait_apart(act, waits_apart)
                for b in range(2):
                    nc.scalar.activation(packed[:, c, g, b * 512:(b + 1) * 512], psum[:, 6 + b, :], ACT.Copy,
                                         bias=65535.0, scale=-1.0).then_inc(packs_free, 1)

            def sqrt_var(n, at, tiles):
                act.wait_ge(var_ready, n)
                nc.scalar.activation(std[:, at:at + tiles], var[:, at:at + tiles], ACT.Sqrt).then_inc(std_ready, 1)

            def save_x1(c):
                act.wait_ge(x1_ready, 2 * c + 2)
                act.dma_start(x1_v[c], nodes[:, bass.ds(c * CT, CT), :]).then_inc(x1_saved, 16)

            def stage_x1(c, n):
                act.wait_ge(x1_ready, 2 * c + n // 2 + 1)
                wait_apart(act, waits_apart)
                nc.scalar.activation(prod[:, n % 2, :, 0:D], nodes[:, bass.ds(c * CT + 2 * n, 2), :],
                                     ACT.Copy).then_inc(x1_staged, 1)

            def store_turned(c, n):
                act.wait_ge(turned_ready, c * QC + n + 1)
                wait_apart(act, waits_apart)
                nc.scalar.activation(hid[:, n % 2, 0:2 * P], bank(acc_bank(c), 0, 0, 2 * P),
                                     ACT.Copy).then_inc(turned_stored, 1)

            def store_h(c, n):
                pair = bank(acc_bank(c), 1 + n % 2, 0, 2 * (D + 2)).rearrange("p (t e) -> p t e", e=D + 2)
                act.wait_ge(h_ready, c * QC + n + 1)
                act.wait_ge(x1_saved, (c + 1) * 16)
                act.wait_ge(x1_staged, c * QC + n + 1)
                wait_apart(act, waits_apart)
                nc.scalar.activation(esed[:, bass.ds(c * CT + 2 * n, 2), :], pair[:, :, D:D + 2], ACT.Copy)
                nc.scalar.activation(nodes[:, bass.ds(c * CT + 2 * n, 2), :], pair[:, :, 0:D],
                                     ACT.Copy).then_inc(h_stored, 1)

            def store_es(c):
                act.wait_ge(h_stored, (c + 1) * QC)
                wait_apart(act, waits_apart)
                nc.scalar.activation(es_col[:], esed[:, bass.ds(c * CT, CT), 0], ACT.Copy).then_inc(es_staged, 1)
                act.wait_ge(es_turned, c + 1)
                act.wait_ge(es_saved, (c + 1) * 16)
                wait_apart(act, waits_apart)
                nc.scalar.activation(es_row, bank(acc_bank(c), 0, 0, P)[0:CT, :], ACT.Copy).then_inc(es_stored, 1)
                act.wait_ge(es_stored, c + 2)
                act.dma_start(es_v[c].rearrange("(t p) -> t p", p=P), es_row).then_inc(es_saved, 16)

            def project_chunk(c):
                stage_x1(c, 0)
                stage_x1(c, 1)
                store_turned(c, 0)
                stage_x1(c, 2)
                store_turned(c, 1)
                store_h(c, 0)
                stage_x1(c, 3)
                store_turned(c, 2)
                store_h(c, 1)
                store_turned(c, 3)
                store_h(c, 2)
                store_h(c, 3)
                store_es(c)

            with act.Fori(0, G) as g:
                take_packs(0, g)
            with act.Fori(1, CH) as c:
                sqrt_var(2 * c - 1, 0, HALF)
                sqrt_var(2 * c, HALF, HALF)
                save_x1(c - 1)
                with act.Fori(0, G - 1) as g:
                    take_packs(c, g)
                project_chunk(c - 1)
                take_packs(c, G - 1)
            sqrt_var(2 * CH - 1, 0, HALF)
            sqrt_var(2 * CH, HALF, HALF)
            save_x1(CH - 1)
            project_chunk(CH - 1)

            act.wait_ge(shift_ready, 2)
            nc.scalar.activation(B_w, esed[:, :, 1], ACT.Exp, bias=shift[:, 0:1])
            nc.scalar.activation(Bp_w, esed[:, :, 1], ACT.Exp, bias=shift[:, 1:2], scale=SLOPE)
            nc.scalar.activation(al_w, w_lo, ACT.Exp)
            nc.scalar.activation(be_w, w_hi, ACT.Exp, scale=-1.0).then_inc(exp_done, 1)
            act.wait_ge(scale_ready, 2)

            def hi_c(jt):
                nc.scalar.activation(rows[:, jt, 0:DE], nodes_ext[:, jt, :], ACT.Copy,
                                     scale=B_w[:, bass.ds(jt, 1)]).then_inc(hi_c_ready, 1)

            def hi_d(jt, b):
                act.wait_ge(prod_d_ready, jt + 1)
                act.wait_ge(rows_c_ready, jt + 1)
                wait_apart(act, waits_apart)
                nc.scalar.activation(rows_d[:, jt, 0:DE], prod[:, 1, b, :], ACT.Copy).then_inc(hi_d_ready, 1)

            def sign_pair(c, r, b):
                at = parity(c) * CW
                m = r * BUFS + b
                act.wait_ge(c_ready, c * TP + m + 1)
                wait_apart(act, waits_apart)
                for k in range(2):
                    nc.scalar.activation(signs[:, b, k * CW:(k + 1) * CW], es_bc[:, bass.ds(at, CW)], ACT.Sign,
                                         bias=esed[:, 2 * m + k, 1:2]).then_inc(signs_ready, 1)

            def scale_d(c):
                act.wait_ge(pairs_used, (c + 1) * TP + BUFS)
                act.wait_ge(out_ready, c + 1)
                wait_apart(act, waits_apart)
                for i in range(CT):
                    nc.scalar.activation(att[:, i, :], psum[:, i, DE:2 * DE], ACT.Copy,
                                         scale=be_w[:, bass.ds(c * CT + i, 1)]).then_inc(d_scaled, 1)

            def normalise(c):
                act.wait_ge(sums_ready, c + 1)
                for i in range(CT):
                    nc.scalar.activation(att[:, i, 0:D], att[:, i, 0:D], ACT.Copy,
                                         scale=rden[:, i:i + 1]).then_inc(norm_done, 1)

            def elu(c):
                act.wait_ge(att_ready, c + 1)
                wait_apart(act, waits_apart)
                nc.scalar.activation(exp_buf(c), att[:, :, 0:D], ACT.Relu, scale=-1.0).then_inc(relu_done, 1)
                act.wait_ge(relu_done, c + 1)
                wait_apart(act, waits_apart)
                nc.scalar.activation(exp_buf(c), exp_buf(c), ACT.Exp, scale=-1.0).then_inc(elu_exp, 1)

            def sqrt1(c):
                sqrt_var(2 * CH + c + 1, 0, CT)

            act.wait_ge(es_landed, 16)
            hi_c(0)
            hi_c(1)
            sign_pair(0, 0, 0)

            def first_pair(m, r, b):
                for n in range(2):
                    hi_c(r * BUFS * 2 + b * 2 + n)
                sign_pair(0, r, b)
                for n in range(2):
                    hi_d(m * 2 + n, n)

            with act.Fori(0, TP // BUFS - 1) as r:
                for b in range(1, BUFS):
                    first_pair(r * BUFS + b - 1, r, b)
                first_pair(r * BUFS + BUFS - 1, r + 1, 0)
            r = TP // BUFS - 1
            for b in range(1, BUFS):
                first_pair(r * BUFS + b - 1, r, b)
            for n in range(2):
                hi_d(T - 2 + n, n)

            with act.Fori(1, CH) as c:
                act.wait_ge(es_landed, (c + 1) * 16)
                pieces = {1: scale_d, 3: normalise, 5: elu, 7: sqrt1}
                for m in range(2 * BUFS):
                    sign_pair(c, m // BUFS, m % BUFS)
                    if m in pieces:
                        pieces[m](c - 1)
                with act.Fori(2, TP // BUFS) as r:
                    for b in range(BUFS):
                        sign_pair(c, r, b)
            for piece in (scale_d, normalise, elu, sqrt1):
                piece(CH - 1)

        @block.vector
        def _(dve):
            dve.sem_inc(c_ready, BUFS)
            dve.sem_inc(acc1_free, CT)
            dve.sem_inc(masks_ready, 1)
            dve.sem_inc(d_ready, 1)
            dve.sem_inc(out_ready, 1)
            consts = Steps(dve, vec_consts)
            consts.did(nc.vector.memset(zeros[:], 0.0))
            consts.did(nc.vector.memset(ones[:], 1.0))
            consts.did(nc.vector.memset(a0_sb[:, 1:2], 1.0))
            consts.did(nc.vector.memset(big[:], 0.0))
            consts.did(nc.vector.memset(nodes_ext[:, :, D], 1.0))
            for k in range(BITS):
                consts.did(nc.vector.memset(bit_w[:, k:k + 1], float(2 ** k)))
            consts.settle()
            dve.sem_inc(consts_ready, 1)

            with dve.Fori(0, Q) as q:
                dve.wait_ge(inp_stored, q + 3)
                nc.vector.tensor_reduce(bits_w[:, bass.ds(q * 4, 4)], nodes[:, bass.ds(q * 4, 4), :], AX.X, ALU.max,
                                        apply_absolute_value=True).then_inc(vec_pro, 1)
            pro = Steps(dve, vec_pro, Q)

            def spread_maxima(n):
                dve.wait_ge(big_turned, n)
                pro.did(nc.vector.tensor_reduce(big_t[:], psum[0:2, 5, 128:256], AX.X, ALU.max))
                pro.settle()
                nc.vector.tensor_scalar(big_d[:], ident[0:2, 0:2], big_t[:, 0:1], None, ALU.mult).then_inc(big_diag, 1)
                dve.wait_ge(big_everywhere, n)

            e_all = psum[:, 4, 0:2 * T].rearrange("p (t two) -> p t two", two=2)
            dve.wait_ge(e_ready, Q + 2)
            nc.vector.tensor_reduce(big[:, 0:1], e_all[:, :, 0], AX.X, ALU.max).then_inc(big_ready, 1)
            dve.wait_ge(consts_ready, 2)
            spread_maxima(1)
            nc.vector.tensor_scalar(shift[:, 0:1], psum[:, 6, 0:1], -1.0, SHIFT, ALU.mult, ALU.add).then_inc(shift_ready, 1)
            dve.wait_ge(exp_done, 1)
            pro.did(nc.vector.scalar_tensor_tensor(out=p_w, in0=e_all[:, :, 1], scalar=0.0, in1=p_w,
                                                   op0=ALU.not_equal, op1=ALU.mult))
            pro.settle()
            pro.did(nc.vector.scalar_tensor_tensor(out=bits_w, in0=bits_w, scalar=1.0, in1=p_w,
                                                   op0=ALU.max, op1=ALU.mult))
            pro.settle()
            pro.did(nc.vector.tensor_scalar(bits_w, bits_w, 2.0 ** -100, None, ALU.max))
            pro.settle()
            pro.did(nc.vector.tensor_scalar(mask_w.bitcast(I32), bits_w.bitcast(I32), EXP_BITS, None, ALU.bitwise_and))
            pro.settle()
            pro.did(nc.vector.tensor_scalar(inv_w.bitcast(I32), mask_w.bitcast(I32), -1.0, float(EXP_TOP),
                                            ALU.mult, ALU.add))
            pro.settle()
            pro.did(nc.vector.scalar_tensor_tensor(out=q_w, in0=inv_w, scalar=PART_TOP, in1=p_w,
                                                   op0=ALU.mult, op1=ALU.mult))
            pro.did(nc.vector.tensor_tensor(pow_w.rearrange("p (g k) -> p g k", k=BITS),
                                            inv_w.rearrange("p (g k) -> p g k", k=BITS),
                                            bit_w[:].rearrange("p (o k) -> p o k", o=1).to_broadcast([P, G, BITS]),
                                            ALU.mult))
            pro.settle()
            pro.did(nc.vector.tensor_copy(rows[:, :, D], q_w))
            pro.settle()
            nc.vector.tensor_tensor(rows[:, :, DE + D], q_w, rows[:, :, D], ALU.subtract).then_inc(scale_ready, 1)

            def make_mask(c, g, k):
                n = (c * G + g) * BITS + k
                jt = g * BITS + k
                mask = seam if k == 0 else adj_in[:, k - 1, 0:CW // 2].bitcast(BF16)
                if k % 2 == 0:
                    dve.wait_ge(adj_landed[k // 2], (c * G + g + 1) * 16)
                dve.wait_ge(masks_used, n + 1)
                dve.wait_ge(masks_ready, n + 1)
                nc.vector.tensor_scalar(mask, adj_in[:, k, :], 0.0, mask_w[:, bass.ds(jt, 1)],
                                        ALU.is_gt, ALU.mult).then_inc(masks_ready, 1)
                nc.vector.tensor_scalar(pack_w[:, k % AHEAD, :], ident_b[:], pow_w[:, bass.ds(jt, 1)], None,
                                        ALU.mult).then_inc(pack_w_ready, 1)

            def ln_stats(steps, tile, at, tiles):
                steps.settle()
                wait_apart(dve, waits_apart)
                for i in range(at, at + tiles):
                    steps.did(nc.vector.bn_stats(stats[:, i, :], tile(i)))
                steps.settle()
                wait_apart(dve, waits_apart)
                for i in range(at, at + tiles):
                    steps.did(nc.vector.bn_aggr(mv[:, i, :], stats[:, i, :]))
                steps.settle()
                nc.vector.tensor_scalar(var[:, at:at + tiles], mv[:, at:at + tiles, 1], EPS, None,
                                        ALU.add).then_inc(var_ready, 1)

            def ln_root(steps, n, at, tiles):
                dve.wait_ge(std_ready, n)
                steps.did(nc.vector.reciprocal(rstd[:, at:at + tiles], std[:, at:at + tiles]))
                steps.settle()

            def ln_apply(tile, at, tiles):
                for i in range(at, at + tiles):
                    last = nc.vector.tensor_scalar(tile(i), tile(i), mv[:, i, 0:1], rstd[:, i:i + 1],
                                                   ALU.subtract, ALU.mult)
                return last

            def node(c):
                return lambda i: nodes[:, c * CT + i, :]

            def divide_weights(steps, c, _):
                dve.wait_ge(masks_used, (c + 1) * T + AHEAD)
                for b in range(3):
                    column = bank(acc_bank(c), b, 0, 3 * DE).rearrange("p (t e) -> p t e", e=DE)[:, :, D]
                    steps.did(nc.vector.tensor_scalar(den[:, 3 * b:3 * b + 3], column, TINY, None, ALU.max))
                steps.settle()
                steps.did(nc.vector.reciprocal(rden[:], den[:]))
                steps.settle()

            def add_x(steps, c, at):
                dve.wait_ge(x_landed, 16)
                for i in (at, at + 1):
                    steps.did(nc.vector.scalar_tensor_tensor(out=nodes[:, c * CT + i, :],
                                                             in0=bank(acc_bank(c), i // 3, (i % 3) * DE, D),
                                                             scalar=rden[:, i:i + 1], in1=nodes[:, c * CT + i, :],
                                                             op0=ALU.mult, op1=ALU.add))

            def stats0(steps, c, half):
                ln_stats(steps, node(c), half * HALF, HALF)

            def apply0(steps, c, at):
                if at % HALF == 0:
                    ln_root(steps, 2 * c + at // HALF + 1, at, HALF)
                last = ln_apply(node(c), at, 2)
                if (at + 2) % HALF == 0:
                    last.then_inc(x1_ready, 1)

            def h_maxima(steps, c, _):
                dve.wait_ge(h_stored, (c + 1) * QC)
                nc.vector.tensor_reduce(h_top[:, bass.ds(c, 1)], nodes[:, bass.ds(c * CT, CT), :], AX.XY, ALU.max,
                                        apply_absolute_value=True).then_inc(h_topped, 1)

            END_STEPS = 3 + 1 + CT + 2 * (CT + 1)
            with dve.Fori(0, G) as g:
                for k in range(BITS):
                    make_mask(0, g, k)
            with dve.Fori(1, CH) as c:
                pieces = {3: (divide_weights, 0), 4: (add_x, 0), 5: (add_x, 2), 6: (add_x, 4), 7: (add_x, 6),
                          8: (stats0, 0), 9: (stats0, 1), 10: (apply0, 0), 11: (apply0, 2), 12: (apply0, 4),
                          13: (apply0, 6)}
                steps = Steps(dve, ln_steps, (c - 1) * END_STEPS)
                for k in range(BITS):
                    make_mask(c, 0, k)
                    if k in pieces:
                        piece, at = pieces[k]
                        piece(steps, c - 1, at)
                assert steps.n == END_STEPS
                if G > 2:
                    with dve.Fori(1, G - 1) as g:
                        for k in range(BITS):
                            make_mask(c, g, k)
                for k in range(BITS):
                    make_mask(c, G - 1, k)
                h_maxima(steps, c - 1, 0)
            steps = Steps(dve, ln_steps, (CH - 1) * END_STEPS)
            for piece, at in ((divide_weights, 0), (add_x, 0), (add_x, 2), (stats0, 0), (add_x, 4), (apply0, 0),
                              (apply0, 2), (add_x, 6), (stats0, 1), (apply0, 4), (apply0, 6), (h_maxima, 0)):
                piece(steps, CH - 1, at)

            mid = Steps(dve, vec_mid)
            mid.did(nc.vector.tensor_reduce(big[:, 0:1], esed[:, :, 1], AX.X, ALU.max))
            dve.wait_ge(h_topped, CH)
            nc.vector.tensor_reduce(big[:, 1:2], h_top[:], AX.X, ALU.max).then_inc(big_ready, 1)
            pro.base, pro.n = pro.base + pro.n, 0
            spread_maxima(2)
            mid.did(nc.vector.tensor_scalar(shift[:, 0:1], psum[:, 6, 0:1], -1.0, None, ALU.mult))
            mid.did(nc.vector.tensor_scalar(shift[:, 1:2], psum[:, 6, 0:1], -SLOPE, None, ALU.mult))
            mid.settle()
            mid.did(nc.vector.tensor_scalar(mask_w, esed[:, :, 0], shift[:, 0:1], 1.0 - SLOPE, ALU.subtract, ALU.mult))
            mid.settle()
            mid.did(nc.vector.tensor_scalar(w_lo, mask_w, 0.0, None, ALU.min))
            nc.vector.tensor_scalar(w_hi, mask_w, 0.0, None, ALU.max).then_inc(shift_ready, 1)
            mid.did(nc.vector.tensor_scalar(shift[:, 2:3], psum[:, 6, 1:2], 1.0, None, ALU.max))
            mid.settle()
            mid.did(nc.vector.tensor_scalar(shift[:, 2:3].bitcast(I32), shift[:, 2:3].bitcast(I32), EXP_BITS, None,
                                            ALU.bitwise_and))
            mid.settle()
            mid.did(nc.vector.tensor_scalar(shift[:, 2:3].bitcast(I32), shift[:, 2:3].bitcast(I32), -1.0,
                                            float(EXP_TOP), ALU.mult, ALU.add))
            mid.settle()
            dve.wait_ge(exp_done, 2)
            mid.did(nc.vector.tensor_scalar(B_w, B_w, shift[:, 2:3], PART_TOP, ALU.mult, ALU.mult))
            nc.vector.tensor_scalar(Bp_w, Bp_w, shift[:, 2:3], PART_TOP, ALU.mult, ALU.mult).then_inc(scale_ready, 1)

            def make_pair(c, g, kk):
                m = (c * G + g) * (BITS // 2) + kk
                b = kk % BUFS
                if isinstance(c, int) and c == 0:
                    for n in range(2):
                        jt = g * BITS + kk * 2 + n
                        dve.wait_ge(hi_c_ready, jt + 1)
                        nc.vector.scalar_tensor_tensor(out=rows[:, jt, DE:2 * DE], in0=nodes_ext[:, jt, :],
                                                       scalar=B_w[:, bass.ds(jt, 1)], in1=rows[:, jt, 0:DE],
                                                       op0=ALU.mult, op1=ALU.subtract).then_inc(rows_c_ready, 1)
                dve.wait_ge(d_ready, m + 1)
                for n in range(2):
                    bit = 2 * kk + n
                    by, way = (14 - bit, ALU.logical_shift_left) if bit <= 14 else (bit - 14, ALU.logical_shift_right)
                    last = nc.vector.tensor_scalar(marks[:, n * CW:(n + 1) * CW].bitcast(U16), packed[:, c, g, :],
                                                   by, ONE_BITS, way, ALU.bitwise_and)
                last.then_inc(marks_ready, 1)
                dve.wait_ge(marks_ready, m + 1)
                dve.wait_ge(signs_ready, 2 * m + 2)
                dve.wait_ge(pairs_used, m + 1)
                nc.vector.tensor_tensor(mask_c[:, b, :], signs[:, b, :], marks, ALU.is_gt).then_inc(c_ready, 1)
                dve.wait_ge(c_ready, m + BUFS + 1)
                nc.vector.tensor_tensor(mask_d[:, b, :], mask_c[:, b, :], marks, ALU.is_equal).then_inc(d_ready, 1)

            def add_c(steps, c):
                for i in range(CT):
                    dve.wait_ge(d_scaled, c * CT + i + 1)
                    nc.vector.scalar_tensor_tensor(out=att[:, i, :], in0=psum[:, i, 0:DE],
                                                   scalar=al_w[:, bass.ds(c * CT + i, 1)], in1=att[:, i, :],
                                                   op0=ALU.mult, op1=ALU.add).then_inc(acc1_free, 1)
                dve.wait_ge(acc1_free, (c + 2) * CT)

                steps.did(nc.vector.tensor_scalar(lone[:], att[:, :, D], 0.0, None, ALU.is_le))
                steps.did(nc.vector.tensor_scalar(den[:, 0:CT], att[:, :, D], TINY, None, ALU.max))
                steps.settle()
                nc.vector.reciprocal(rden[:, 0:CT], den[:, 0:CT]).then_inc(sums_ready, 1)

            def x1_tile(c):
                return lambda i: x1_buf(c)[:, i, :]

            def add_elu(steps, c):
                dve.wait_ge(elu_exp, c + 1)
                dve.wait_ge(att_ready, c + 1)
                steps.did(nc.vector.scalar_tensor_tensor(out=exp_buf(c), in0=att[:, :, 0:D], scalar=0.0, in1=exp_buf(c),
                                                         op0=ALU.max, op1=ALU.add))
                steps.settle()
                dve.wait_ge(x1_landed, (c + 1) * 16)
                steps.did(nc.vector.scalar_tensor_tensor(out=x1_buf(c), in0=exp_buf(c), scalar=-1.0, in1=x1_buf(c),
                                                         op0=ALU.add, op1=ALU.add))
                ln_stats(steps, x1_tile(c), 0, CT)

            def finish(steps, c):
                ln_root(steps, 2 * CH + c + 1, 0, CT)
                ln_apply(x1_tile(c), 0, CT).then_inc(out_ready, 1)

            OUT_STEPS = 2 + 2 + 2 * CT + 1
            for kk in range(BITS // 2):
                make_pair(0, 0, kk)
            with dve.Fori(1, G) as g:
                for kk in range(BITS // 2):
                    make_pair(0, g, kk)
            with dve.Fori(1, CH) as c:
                steps = Steps(dve, out1_steps, (c - 1) * OUT_STEPS)
                pieces = {1: add_c, 5: add_elu, 7: finish}
                for kk in range(BITS // 2):
                    make_pair(c, 0, kk)
                    if kk in pieces:
                        pieces[kk](steps, c - 1)
                assert steps.n == OUT_STEPS
                with dve.Fori(1, G) as g:
                    for kk in range(BITS // 2):
                        make_pair(c, g, kk)
            steps = Steps(dve, out1_steps, (CH - 1) * OUT_STEPS)
            for piece in (add_c, add_elu, finish):
                piece(steps, CH - 1)

        @block.gpsimd
        def _(pool):
            own = Steps(pool, pool_steps)
            own.did(nc.gpsimd.memset(ident[:], 0.0))
            own.settle()
            own.did(nc.gpsimd.affine_select(out=ident[:], in_=ident[:], compare_op=ALU.not_equal, fill=1.0,
                                            base=0, pattern=[[-1, P]], channel_multiplier=1))
            own.settle()
            nc.gpsimd.tensor_copy(ident_b[:], ident[:]).then_inc(consts_ready, 1)

            pool.wait_ge(scale_ready, 1)
            with pool.Fori(0, T // 2) as r:
                for b in range(2):
                    jt = r * 2 + b
                    nc.gpsimd.tensor_tensor(prod[:, 0, b, 0:D], nodes[:, jt, :],
                                            q_w[:, bass.ds(jt, 1)].to_broadcast([P, D]), ALU.mult).then_inc(prod_ready, 1)
                    pool.wait_ge(prod_ready, jt + 1)
                    pool.wait_ge(hi_ready, jt + 1)
                    wait_apart(pool, waits_apart)
                    nc.gpsimd.tensor_tensor(rows[:, jt, DE:DE + D], prod[:, 0, b, 0:D], rows[:, jt, 0:D],
                                            ALU.subtract).then_inc(rows_ready, 1)
                    pool.wait_ge(rows_ready, jt + 1)
                    wait_apart(pool, waits_apart)

            nc.gpsimd.memset(hsum[:], 0.0).then_inc(hsum_steps, 1)
            with pool.Fori(0, CH) as c:
                pool.wait_ge(h_stored, (c + 1) * QC)
                for i in range(CT):
                    pool.wait_ge(hsum_steps, c * CT + i + 1)
                    wait_apart(pool, waits_apart)
                    nc.gpsimd.tensor_tensor(hsum[:], hsum[:], nodes[:, c * CT + i, :], ALU.add).then_inc(hsum_steps, 1)

            def product_d(jt, b):
                nc.gpsimd.tensor_tensor(prod[:, 1, b, :], nodes_ext[:, jt, :],
                                        Bp_w[:, bass.ds(jt, 1)].to_broadcast([P, DE]), ALU.mult).then_inc(prod_d_ready, 1)

            def lo_d(jt, b):
                pool.wait_ge(prod_d_ready, jt + 1)
                pool.wait_ge(hi_d_ready, jt + 1)
                wait_apart(pool, waits_apart)
                nc.gpsimd.tensor_tensor(rows_d[:, jt, DE:2 * DE], prod[:, 1, b, :], rows_d[:, jt, 0:DE],
                                        ALU.subtract).then_inc(rows1_ready, 1)
                pool.wait_ge(rows1_ready, jt + 1)
                wait_apart(pool, waits_apart)

            pool.wait_ge(hsum_steps, T + 1)
            pool.wait_ge(scale_ready, 2)
            product_d(0, 0)
            with pool.Fori(0, T // 2 - 1) as r:
                for b in range(2):
                    product_d(r * 2 + b + 1, 1 - b)
                    lo_d(r * 2 + b, b)
            product_d(T - 1, 1)
            lo_d(T - 2, 0)
            lo_d(T - 1, 1)

            nc.gpsimd.partition_all_reduce(hmean, hsum[:], P, bass.bass_isa.ReduceOp.add).then_inc(mean_steps, 1)
            pool.wait_ge(mean_steps, 1)
            nc.gpsimd.tensor_scalar(hmean, hmean, 1.0 / N, 1.0, ALU.mult, ALU.mult).then_inc(hmean_ready, 1)

            pool.wait_ge(hmean_ready, 1)
            with pool.Fori(0, CH) as c:
                for i in range(CT):
                    pool.wait_ge(norm_done, c * CT + i + 1)
                    nc.gpsimd.tensor_tensor(prod[:, 0, i % 2, 0:D], hmean, lone[:, i:i + 1].to_broadcast([P, D]),
                                            ALU.mult).then_inc(mean_steps, 1)
                    pool.wait_ge(mean_steps, c * CT + i + 2)
                    last = nc.gpsimd.tensor_tensor(att[:, i, 0:D], att[:, i, 0:D], prod[:, 0, i % 2, 0:D], ALU.add)
                last.then_inc(att_ready, 1)


def kernel(x, adj, L0_gnn_W, L0_gnn_b, L0_gnn_a, L1_gnn_W, L1_gnn_a):
    import numpy as np
    import concourse.bacc as bacc
    from concourse.bass_utils import run_bass_kernel_spmd

    x, adj, W1 = np.asarray(x), np.asarray(adj), np.asarray(L1_gnn_W)
    N = x.shape[0]
    blocks = adj.reshape(N // CW, CW, N // (2 * P), 2, P).transpose(0, 2, 4, 3, 1)
    arrays = {
        "x": x, "xT": x.T, "adj_blocks": blocks.reshape(-1, P, 2, CW),
        "W0": np.asarray(L0_gnn_W), "b0": np.asarray(L0_gnn_b), "a0": np.asarray(L0_gnn_a),
        "W1": W1, "W1T": W1.T, "a1": np.asarray(L1_gnn_a).reshape(2, D).T,
    }
    arrays = {name: np.ascontiguousarray(a) for name, a in arrays.items()}

    nc = bacc.Bacc("TRN2", target_bir_lowering=False, num_devices=1)
    aps = [nc.dram_tensor(name, a.shape, mybir.dt.from_np(a.dtype), kind="ExternalInput").ap()
           for name, a in arrays.items()]
    es_dram = nc.dram_tensor("es_by_node", (N,), F32, kind="Internal").ap()
    x1_dram = nc.dram_tensor("x1", (N, D), F32, kind="Internal").ap()
    out = nc.dram_tensor("out", (N, D), F32, kind="ExternalOutput").ap()
    gat_kernel(nc, *aps, es_dram, x1_dram, out)
    return run_bass_kernel_spmd(nc, [arrays], core_ids=[0]).results[0]["out"]
```

```python
from contextlib import ExitStack

import concourse.bass as bass
from concourse import mybir

P = 128
D = 128
BITS = 16
CT = 8
CW = CT * P
DE = D + 1
AHEAD = 4
XBUF = 4
SLOTS = 8
EARLY = 3
HALF = CT // 2
BUFS = 4
EPS = 1e-5
SLOPE = 0.01
SHIFT = 30.0
TINY = 1e-37
ONE_BITS = 0x4000
EXP_BITS = 0x7F800000
EXP_TOP = 0x7F000000
PART_TOP = 2.0 ** 14

ALU = mybir.AluOpType
ACT = mybir.ActivationFunctionType
F32 = mybir.dt.float32
F16 = mybir.dt.float16
BF16 = mybir.dt.bfloat16
I32 = mybir.dt.int32
U16 = mybir.dt.uint16
AX = mybir.AxisListType


def wait_apart(engine, waits_apart):
    engine.sem_inc(waits_apart, 1)


class Steps:

    def __init__(self, engine, sem, base=0):
        self.engine, self.sem, self.base, self.n = engine, sem, base, 0

    def did(self, instruction):
        instruction.then_inc(self.sem, 1)
        self.n += 1

    def settle(self):
        self.engine.wait_ge(self.sem, self.base + self.n)


def gat_kernel(nc, x, xT, adj_blocks, W0, b0, a0, W1, W1T, a1, es_dram, x1_dram, out):
    N = x.shape[0]
    T = N // P
    CH = N // CW
    G = T // BITS
    Q = N // 512
    TP = T // 2
    QC = CT // 2
    LAST_TURN = CH * T - BITS + AHEAD
    assert G == 4 and Q % XBUF == 0

    x_v = x.rearrange("(t p) d -> p t d", p=P)
    out_v = out.rearrange("(c t p) d -> c p t d", p=P, t=CT)
    x1_v = x1_dram.rearrange("(c t p) d -> c p t d", p=P, t=CT)
    es_v = es_dram.rearrange("(c w) -> c w", w=CW)

    with ExitStack() as ctx:
        def sb(name, shape, dt):
            return ctx.enter_context(nc.sbuf_tensor(name, shape, dt))

        def sem(name):
            return ctx.enter_context(nc.semaphore(name))

        psum = ctx.enter_context(nc.psum_tensor("psum", [P, 8, 512], F32))

        rows = sb("rows", [P, T, 2 * DE], F16)
        packed = sb("packed", [P, CH * G, CW], U16)
        xT_sb = packed[:].rearrange("p g w -> p (g w)")[:, 0:XBUF * 2 * 512].bitcast(F32).rearrange(
            "p (b n) -> p b n", b=XBUF)
        nodes_ext = sb("nodes", [P, T, DE], F32)
        nodes = nodes_ext[:, :, 0:D]
        rows_d = nodes_ext[:].rearrange("p t e -> p (t e)").bitcast(F16).rearrange("p (t e) -> p t e", e=2 * DE)
        arena = sb("arena", [P, 2 * SLOTS * CW + CW // 2], I32)
        adj_in = arena[:, 0:2 * SLOTS * CW].rearrange("p (t w) -> p t w", w=CW)
        seam = arena[:, 2 * SLOTS * CW:2 * SLOTS * CW + CW // 2].bitcast(BF16)
        es_bc = arena[:, 0:2 * CW].bitcast(F32)
        marks = arena[:, 2 * CW:4 * CW].bitcast(BF16).rearrange("p (b w) -> p b w", w=2 * CW)
        signs, mask_c, mask_d = (
            arena[:, (4 + n * BUFS) * CW:(4 + (n + 1) * BUFS) * CW].bitcast(BF16).rearrange("p (b w) -> p b w", w=2 * CW)
            for n in range(3))

        att = sb("att", [P, CT, DE], F32)
        hid = att[:].rearrange("p t e -> p (t e)")[:, 0:2 * 512].rearrange("p (b n) -> p b n", b=2)

        def over_packed(word):
            return packed[:, bass.ds(word, 2), :].rearrange("p g w -> p (g w)").bitcast(F32).rearrange(
                "p (t d) -> p t d", d=D)

        def x_buf(c):
            return over_packed(CH * G // 2 + 2 * c)

        x_early = packed[:, CH * G // 2:, :].rearrange("p g w -> p (g w)").bitcast(F32).rearrange(
            "p (t d) -> p t d", d=D)

        adj_early = packed[:, G:(EARLY + 1) * G, :].rearrange("p g w -> p (g w)").bitcast(I32).rearrange(
            "p (t w) -> p t w", w=CW)

        def exp_buf(c):
            return over_packed(c * G)

        def x1_buf(c):
            return over_packed(c * G + 2)

        ident = sb("ident", [P, P], F32)
        ident_b = sb("ident_b", [P, P], BF16)
        zeros = sb("zeros", [P, P], BF16)
        ones = sb("ones", [2, 1], F32)
        pack_w = sb("pack_w", [P, AHEAD, P], BF16)
        W0_sb = sb("W0_sb", [P, D], F32)
        b0_sb = sb("b0_sb", [P, 1], F32)
        a0_sb = sb("a0_sb", [P, 2], F32)
        W1_sb = sb("W1_sb", [P, D + 2], F32)
        W1T_sb = sb("W1T_sb", [P, D], F32)
        a1_sb = sb("a1_sb", [P, 2], F32)
        bit_w = sb("bit_w", [P, BITS], F32)
        big = sb("big", [P, 2], F32)
        big_t = sb("big_t", [2, 1], F32)
        big_d = sb("big_d", [2, 2], F32)
        shift = sb("shift", [P, 4], F32)
        wt = sb("wt", [P, 6, T], F32)
        p_w, q_w, mask_w, inv_w, pow_w, bits_w = (wt[:, n, :] for n in range(6))
        B_w, Bp_w, al_w, be_w, w_lo, w_hi = (wt[:, n, :] for n in range(6))
        esed = sb("esed", [P, T, 2], F32)
        es_row = W1T_sb[0:CT, :]
        es_col = sb("es_col", [P, CT], F32)
        prod = sb("prod", [P, 2, 2, DE], F32)
        hsum = sb("hsum", [P, D], F32)
        hmean = W1T_sb[:]
        h_top = sb("h_top", [P, 2 * CH], F32)
        den = sb("den", [P, 9], F32)
        rden = sb("rden", [P, 9], F32)
        c_weights = sb("c_weights", [P, CT], F32)
        lone = sb("lone", [P, CT], F32)
        stats = sb("stats", [P, CT, 6], F32)
        mv = sb("mv", [P, CT, 2], F32)
        var = sb("var", [P, CT], F32)
        std = sb("std", [P, CT], F32)
        idle = sb("idle", [P, 1], F32)
        rstd = sb("rstd", [P, CT], F32)

        banks = psum[:].rearrange("p b n -> p (b n)")

        def bank(first, n, at, width):
            return banks[:, bass.ds(first * 512 + (n * 512 + at), width)]

        def parity(c):
            return c % 2 if isinstance(c, int) else c & 1

        def acc_bank(c):
            return parity(c) * 3

        xT_landed = [sem(f"xT_landed{b}") for b in range(XBUF)]
        W0_landed = sem("W0_landed")
        weights_landed = sem("weights_landed")
        W1_landed = sem("W1_landed")
        early_landed = sem("early_landed")
        adj_landed = [sem(f"adj_landed{s}") for s in range(SLOTS)]
        x_landed = sem("x_landed")
        last_x_landed = sem("last_x_landed")
        consts_ready = sem("consts_ready")
        waits_apart = sem("waits_apart")
        pool_steps = sem("pool_steps")
        vec_consts = sem("vec_consts")
        hidden_ready = sem("hidden_ready")
        tanh_done = sem("tanh_done")
        e_ready = sem("e_ready")
        inp_ready = sem("inp_ready")
        inp_stored = sem("inp_stored")
        vec_pro = sem("vec_pro")
        vec_mid = sem("vec_mid")
        big_ready = sem("big_ready")
        big_turned = sem("big_turned")
        big_diag = sem("big_diag")
        big_everywhere = sem("big_everywhere")
        shift_ready = sem("shift_ready")
        exp_done = sem("exp_done")
        scale_ready = sem("scale_ready")
        hi_ready = sem("hi_ready")
        prod_ready = sem("prod_ready")
        rows_ready = sem("rows_ready")
        masks_ready = sem("masks_ready")
        masks_used = sem("masks_used")
        pack_w_ready = sem("pack_w_ready")
        packs_ready = sem("packs_ready")
        packs_free = sem("packs_free")
        ln_steps = sem("ln_steps")
        var_ready = sem("var_ready")
        std_ready = sem("std_ready")
        x1_ready = sem("x1_ready")
        wa_ready = sem("wa_ready")
        wa_stored = sem("wa_stored")
        x1_staged = sem("x1_staged")
        turned_ready = sem("turned_ready")
        turned_stored = sem("turned_stored")
        h_ready = sem("h_ready")
        h_stored = sem("h_stored")
        h_ones = sem("h_ones")
        es_turned = sem("es_turned")
        es_stored = sem("es_stored")
        es_staged = sem("es_staged")
        es_saved = sem("es_saved")
        x1_saved = [sem(f"x1_saved{half}") for half in range(2)]
        x1_landed = sem("x1_landed")
        h_topped = sem("h_topped")
        es_landed = sem("es_landed")
        signs_ready = sem("signs_ready")
        marks_ready = sem("marks_ready")
        c_ready = sem("c_ready")
        d_ready = sem("d_ready")
        hsum_steps = sem("hsum_steps")
        pairs_used = sem("pairs_used")
        hi_c_ready = sem("hi_c_ready")
        sums_ready = sem("sums_ready")
        norm_done = sem("norm_done")
        prod_d_ready = sem("prod_d_ready")
        hi_d_ready = sem("hi_d_ready")
        rows_c_ready = sem("rows_c_ready")
        rows1_ready = sem("rows1_ready")
        mean_steps = sem("mean_steps")
        hmean_ready = sem("hmean_ready")
        d_scaled = sem("d_scaled")
        c_taken = sem("c_taken")
        out1_steps = sem("out1_steps")
        att_ready = sem("att_ready")
        relu_done = sem("relu_done")
        elu_exp = sem("elu_exp")
        out_ready = sem("out_ready")
        out_stored = sem("out_stored")

        WEIGHT_DMAS = 2
        W1_DMAS = 3
        block = ctx.enter_context(nc.Block())

        @block.sync
        def _(sp):
            def load_xT(q, b):
                sp.dma_start(xT_sb[:, b, :], xT[:, bass.ts(q, 512)]).then_inc(xT_landed[b], 16)

            def load_x(n):
                first, end = ((T - CT) * k // 3 for k in (n, n + 1))
                sp.dma_start(x_early[:, first:end, :], x_v[:, first:end, :]).then_inc(x_landed, 16)

            def load_pair(pair, slot):
                sp.dma_start(adj_in[:, 2 * slot:2 * slot + 2, :], adj_blocks[pair]).then_inc(adj_landed[slot], 16)

            sp.dma_start(W0_sb[:], W0).then_inc(W0_landed, 16)
            for b in range(XBUF):
                load_xT(b, b)
            load_x(0)
            slots = list(range(SLOTS))
            for q in range(XBUF, Q):
                sp.wait_ge(inp_ready, q - XBUF + 1)
                load_xT(q, q % XBUF)
                n = (q - XBUF) // 2
                if q % 2 == 0:
                    if n < 2:
                        load_x(n + 1)
                    else:
                        load_pair(slots[0], slots.pop(0))
            for slot in slots:
                load_pair(slot, slot)
            for n in range(EARLY):
                sp.dma_start(adj_early[:, 2 * n:2 * n + 2, :], adj_blocks[2 * SLOTS - EARLY + n]).then_inc(early_landed, 16)

            def load_turn(r, slots=SLOTS):
                for slot in range(slots):
                    sp.wait_ge(masks_used, (r - 1) * BITS + min(2 * slot + 3, BITS) + AHEAD)
                    load_pair(r * SLOTS + slot, slot)

            load_turn(1, SLOTS - EARLY)
            sp.wait_ge(early_landed, EARLY * 16)
            for slot in range(SLOTS - EARLY, SLOTS):
                sp.sem_inc(adj_landed[slot], 16)
            with sp.Fori(2, CH * G) as r:
                load_turn(r)

            def load_es(c):
                if not isinstance(c, int):
                    sp.wait_ge(signs_ready, (c - 1) * T)
                if not (isinstance(c, int) and c == 0):
                    sp.wait_ge(es_landed, c * 16)
                    wait_apart(sp, waits_apart)
                sp.dma_start(es_bc[:, bass.ds(parity(c) * CW, CW)], es_v[c].partition_broadcast(P)).then_inc(es_landed, 16)

            def load_x1(c):
                sp.wait_ge(marks_ready, (c + 1) * TP)
                wait_apart(sp, waits_apart)
                sp.dma_start(x1_buf(c), x1_v[c]).then_inc(x1_landed, 16)

            def store_out(c):
                sp.wait_ge(out_ready, 2 * c + 3)
                sp.dma_start(out_v[c], x1_buf(c)).then_inc(out_stored, 16)

            sp.wait_ge(masks_used, LAST_TURN + 3)
            sp.wait_ge(es_saved, 16 * 3)
            load_es(0)
            load_es(1)
            sp.wait_ge(es_saved, 16 * (CH + 1))
            for half in range(2):
                sp.wait_ge(x1_saved[half], 16 * CH)
            if CH > 2:
                with sp.Fori(1, CH - 1) as c:
                    load_x1(c - 1)
                    load_es(c + 1)
                    store_out(c - 1)
            load_x1(CH - 2)
            store_out(CH - 2)
            load_x1(CH - 1)
            for half in range(2):
                sp.wait_ge(out_ready, 2 * CH + half)
                tiles = slice(half * HALF, (half + 1) * HALF)
                sp.dma_start(out_v[CH - 1][:, tiles, :], x1_buf(CH - 1)[:, tiles, :]).then_inc(out_stored, 16)
            sp.wait_ge(out_stored, 16 * (CH + 1))

        @block.tensor
        def _(pe):
            pe.sem_inc(e_ready, 2)
            pe.sem_inc(masks_used, AHEAD)
            pe.sem_inc(pairs_used, BUFS)
            pe.wait_ge(W0_landed, 16)

            def hidden(q, xb):
                pe.wait_ge(tanh_done, q + 1)
                nc.tensor.matmul(psum[:, xb % 2, :], W0_sb[:], xT_sb[:, xb, :],
                                 start=True, stop=True).then_inc(hidden_ready, 1)

            def inputs(q, xb):
                pe.wait_ge(inp_stored, q + 1)
                for n in range(4):
                    last = nc.tensor.matmul(psum[:, 2 + xb % 2, n * D:(n + 1) * D], xT_sb[:, xb, n * P:(n + 1) * P],
                                            W0_sb[:], start=True, stop=True, skip_group_check=True)
                last.then_inc(inp_ready, 1)

            def scores(q, b):
                pe.wait_ge(tanh_done, q + 3)
                for n in range(4):
                    last = nc.tensor.matmul(psum[:, 4, bass.ds((q * 4 + n) * 2, 2)], hid[:, b, n * P:(n + 1) * P],
                                            a0_sb[:], start=True, stop=True, skip_group_check=True)
                last.then_inc(e_ready, 1)

            def first_step(q, xb, landed, before):
                pe.wait_ge(xT_landed[xb], landed * 16)
                hidden(q, xb)
                if before is not None:
                    scores(before, (xb + 1) % 2)
                inputs(q, xb)

            for xb in range(XBUF):
                if xb == 1:
                    pe.wait_ge(weights_landed, 16 * WEIGHT_DMAS)
                    pe.wait_ge(consts_ready, 2)
                first_step(xb, xb, 1, xb - 1 if xb else None)
            with pe.Fori(1, Q // XBUF) as r:
                for xb in range(XBUF):
                    first_step(r * XBUF + xb, xb, r + 1, r * XBUF + xb - 1)
            scores(Q - 1, 1)

            pe.wait_ge(W1_landed, 16 * W1_DMAS)
            nc.tensor.matmul(psum[:, 7, 0:2], W1T_sb[:], a1_sb[:], start=True, stop=True).then_inc(wa_ready, 1)

            def spread_maxima(n):
                pe.wait_ge(big_ready, n)
                nc.tensor.transpose(psum[0:2, 5, 128:256], big[:], ident[:]).then_inc(big_turned, 1)
                pe.wait_ge(big_diag, n)
                nc.tensor.matmul(psum[:, 6, 0:2], ones[:].to_broadcast([2, P]), big_d[:], start=True, stop=True).then_inc(big_everywhere, 1)

            spread_maxima(1)

            zero_moving = zeros[:, 0:1]
            pe.wait_ge(exp_done, 1)
            pe.wait_ge(scale_ready, 1)
            pe.wait_ge(inp_stored, Q + 2)
            pe.wait_ge(wa_stored, 1)

            def open_sums(c):
                for n in range(3):
                    nc.tensor.matmul(bank(acc_bank(c), n, 0, 3 * DE), zeros[:], zero_moving.to_broadcast([P, 3 * DE]),
                                     start=True, stop=False, skip_group_check=True)

            def add_tiles(c, g, between={}):
                for k in range(BITS):
                    jt = g * BITS + k
                    mask = seam if k == 0 else adj_in[:, k - 1, 0:CW // 2].bitcast(BF16)
                    pe.wait_ge(masks_ready, (c * G + g) * BITS + k + 2)
                    pe.wait_ge(rows_ready, jt + 1)
                    for i in range(CT):
                        for part in range(2):
                            nc.tensor.matmul(bank(acc_bank(c), i // 3, (i % 3) * DE, DE), mask[:, i * P:(i + 1) * P],
                                             rows[:, jt, part * DE:(part + 1) * DE],
                                             start=False, stop=True, skip_group_check=True)
                    pe.wait_ge(pack_w_ready, (c * G + g) * BITS + k + 1)
                    for b in range(2):
                        if k == 0:
                            pe.wait_ge(packs_free, (c * G + g) * 2 + b + 1)
                        last = nc.tensor.matmul(psum[:, 6 + b, :], pack_w[:, k % AHEAD, :],
                                                mask[:, b * 512:(b + 1) * 512],
                                                start=(k == 0), stop=(k == BITS - 1))
                    last.then_inc(masks_used, 1)
                    for step, n in between.get(k, ()):
                        step(c - 1, n)

            def turn(c, n):
                pe.wait_ge(x1_staged, c * QC + n + 1)
                pe.wait_ge(turned_stored, c * QC + n + 1)
                wait_apart(pe, waits_apart)
                for t in range(2):
                    last = nc.tensor.matmul(bank(acc_bank(c), 0, t * P, P), prod[:, n % 2, t, 0:D], ident[:],
                                            start=True, stop=True, skip_group_check=True)
                last.then_inc(turned_ready, 1)

            def project(c, n):
                pe.wait_ge(turned_stored, c * QC + n + 2)
                if n >= 2:
                    pe.wait_ge(h_stored, c * QC + n - 1)
                for t in range(2):
                    last = nc.tensor.matmul(bank(acc_bank(c), 1 + n % 2, t * (D + 2), D + 2),
                                            hid[:, n % 2, t * P:(t + 1) * P], W1_sb[:],
                                            start=True, stop=True, skip_group_check=True)
                last.then_inc(h_ready, 1)

            def turn_es(c, n):
                pe.wait_ge(es_staged, c + 1)
                wait_apart(pe, waits_apart)
                nc.tensor.matmul(bank(acc_bank(c), 0, 0, P)[0:CT, :], es_col[:], ident[:], start=True, stop=True,
                                 skip_group_check=True).then_inc(es_turned, 1)

            open_sums(0)
            with pe.Fori(0, G) as g:
                add_tiles(0, g)
            with pe.Fori(1, CH) as c:
                pe.wait_ge(es_stored, c)
                open_sums(c)
                with pe.Fori(0, G - 1) as g:
                    add_tiles(c, g)
                add_tiles(c, G - 1, {0: [(turn, 0)], 2: [(turn, 1)], 3: [(project, 0)], 5: [(turn, 2)],
                                     6: [(project, 1)], 8: [(turn, 3)], 9: [(project, 2)], 11: [(project, 3)],
                                     13: [(turn_es, 0)]})
            for step, n in ((turn, 0), (turn, 1), (project, 0), (turn, 2), (project, 1), (turn, 3), (project, 2),
                            (project, 3), (turn_es, 0)):
                step(CH - 1, n)

            spread_maxima(2)

            pe.wait_ge(packs_free, 2 * CH * G + 2)
            pe.wait_ge(es_stored, CH + 1)
            pe.wait_ge(scale_ready, 2)
            def open_bank(c, i):
                pe.wait_ge(d_scaled, c * CT + i + 1)
                nc.tensor.matmul(psum[:, i, 0:3 * DE], zeros[:], zero_moving.to_broadcast([P, 3 * DE]),
                                 start=True, stop=False, skip_group_check=True)

            def add_pair(c, m, b, opening=False):
                pe.wait_ge(d_ready, c * TP + m + 2)
                for n in range(2):
                    jt = m * 2 + n
                    pe.wait_ge(rows1_ready, jt + 1)
                    for i in range(CT):
                        at = n * CW + i * P
                        if opening and n == 0:
                            open_bank(c, i)
                        nc.tensor.matmul(psum[:, i, 0:2 * DE], mask_c[:, b, at:at + P], rows[:, jt, :],
                                         start=False, stop=True, skip_group_check=True)
                        for part in range(2):
                            last = nc.tensor.matmul(psum[:, i, 2 * DE:3 * DE], mask_d[:, b, at:at + P],
                                                    rows_d[:, jt, part * DE:(part + 1) * DE],
                                                    start=False, stop=True, skip_group_check=True)
                last.then_inc(pairs_used, 1)

            with pe.Fori(0, CH) as c:
                for b in range(BUFS):
                    add_pair(c, b, b, opening=(b == 0))
                with pe.Fori(1, TP // BUFS) as r:
                    for b in range(BUFS):
                        add_pair(c, r * BUFS + b, b)

        @block.scalar
        def _(act):
            act.sem_inc(tanh_done, 2)
            act.sem_inc(inp_stored, 2)
            act.sem_inc(packs_free, 2)
            act.sem_inc(d_scaled, CT)
            act.sem_inc(turned_stored, 1)
            act.sem_inc(es_stored, 1)
            act.sem_inc(es_saved, 16)
            for dst, src in ((b0_sb[:], b0.rearrange("(d o) -> d o", o=1)), (a0_sb[:, 0:1], a0)):
                act.dma_start(dst, src).then_inc(weights_landed, 16)
            for dst, src in ((W1_sb[:, 0:D], W1), (W1T_sb[:], W1T), (a1_sb[:], a1)):
                act.dma_start(dst, src).then_inc(W1_landed, 16)
            act.wait_ge(weights_landed, 16 * WEIGHT_DMAS)

            with act.Fori(0, Q // XBUF) as r:
                for n in range(XBUF):
                    q, b = r * XBUF + n, n % 2
                    act.wait_ge(hidden_ready, q + 1)
                    act.wait_ge(e_ready, q + 1)
                    nc.scalar.activation(hid[:, b, :], psum[:, b, :], ACT.Tanh, bias=b0_sb[:, 0:1]).then_inc(tanh_done, 1)
                    act.wait_ge(inp_ready, q + 1)
                    wait_apart(act, waits_apart)
                    nc.scalar.activation(nodes[:, bass.ds(q * 4, 4), :],
                                         psum[:, 2 + b, :].rearrange("p (t d) -> p t d", d=D), ACT.Copy).then_inc(inp_stored, 1)

            act.wait_ge(wa_ready, 1)
            nc.scalar.activation(W1_sb[:, D:D + 2], psum[:, 7, 0:2], ACT.Copy).then_inc(wa_stored, 1)

            act.wait_ge(shift_ready, 1)
            nc.scalar.activation(p_w, psum[:, 4, 0:2 * T].rearrange("p (t two) -> p t two", two=2)[:, :, 0], ACT.Exp,
                                 bias=shift[:, 0:1]).then_inc(exp_done, 1)

            act.wait_ge(scale_ready, 1)
            with act.Fori(0, T // 4) as r:
                for n in range(4):
                    nc.scalar.activation(rows[:, r * 4 + n, 0:D], nodes[:, r * 4 + n, :], ACT.Copy,
                                         scale=q_w[:, bass.ds(r * 4 + n, 1)]).then_inc(hi_ready, 1)

            def take_packs(c, g):
                act.wait_ge(masks_used, (c * G + g + 1) * BITS + AHEAD)
                wait_apart(act, waits_apart)
                for b in range(2):
                    nc.scalar.activation(packed[:, c * G + g, b * 512:(b + 1) * 512], psum[:, 6 + b, :], ACT.Copy,
                                         bias=65535.0, scale=-1.0).then_inc(packs_free, 1)

            def sqrt_var(n, at, tiles):
                act.wait_ge(var_ready, n)
                nc.scalar.activation(std[:, at:at + tiles], var[:, at:at + tiles], ACT.Sqrt).then_inc(std_ready, 1)

            def save_x1(c, half):
                act.wait_ge(x1_ready, 2 * c + half + 1)
                tiles = slice(half * HALF, (half + 1) * HALF)
                act.dma_start(x1_v[c][:, tiles, :], nodes[:, bass.ds(c * CT + half * HALF, HALF), :]).then_inc(
                    x1_saved[half], 16)

            def stage_x1(c, n):
                act.wait_ge(x1_ready, 2 * c + n // 2 + 1)
                wait_apart(act, waits_apart)
                nc.scalar.activation(prod[:, n % 2, :, 0:D], nodes[:, bass.ds(c * CT + 2 * n, 2), :],
                                     ACT.Copy).then_inc(x1_staged, 1)

            def store_turned(c, n):
                act.wait_ge(turned_ready, c * QC + n + 1)
                wait_apart(act, waits_apart)
                nc.scalar.activation(hid[:, n % 2, 0:2 * P], bank(acc_bank(c), 0, 0, 2 * P),
                                     ACT.Copy).then_inc(turned_stored, 1)

            def store_h(c, n):
                pair = bank(acc_bank(c), 1 + n % 2, 0, 2 * (D + 2)).rearrange("p (t e) -> p t e", e=D + 2)
                act.wait_ge(h_ready, c * QC + n + 1)
                act.wait_ge(x1_saved[n // 2], (c + 1) * 16)
                act.wait_ge(x1_staged, c * QC + n + 1)
                wait_apart(act, waits_apart)
                nc.scalar.activation(esed[:, bass.ds(c * CT + 2 * n, 2), :], pair[:, :, D:D + 2], ACT.Copy)
                nc.scalar.activation(nodes[:, bass.ds(c * CT + 2 * n, 2), :], pair[:, :, 0:D],
                                     ACT.Copy).then_inc(h_stored, 1)

            def store_es(c):
                act.wait_ge(h_stored, (c + 1) * QC)
                wait_apart(act, waits_apart)
                nc.scalar.activation(es_col[:], esed[:, bass.ds(c * CT, CT), 0], ACT.Copy).then_inc(es_staged, 1)
                act.wait_ge(es_turned, c + 1)
                act.wait_ge(es_saved, (c + 1) * 16)
                wait_apart(act, waits_apart)
                nc.scalar.activation(es_row, bank(acc_bank(c), 0, 0, P)[0:CT, :], ACT.Copy).then_inc(es_stored, 1)
                act.wait_ge(es_stored, c + 2)
                act.dma_start(es_v[c].rearrange("(t p) -> t p", p=P), es_row).then_inc(es_saved, 16)

            def project_chunk(c, turned=0):
                if not turned:
                    store_turned(c, 0)
                stage_x1(c, 2)
                store_turned(c, 1)
                store_h(c, 0)
                stage_x1(c, 3)
                store_turned(c, 2)
                store_h(c, 1)
                store_turned(c, 3)
                store_h(c, 2)
                store_h(c, 3)
                store_es(c)

            with act.Fori(0, G) as g:
                take_packs(0, g)
            act.wait_ge(rows_ready, T)
            act.dma_start(nodes[:, T - CT:, :], x_v[:, T - CT:, :]).then_inc(last_x_landed, 16)

            def bring_exp():
                nc.scalar.activation(idle[:], b0_sb[:], ACT.Exp)

            def end_of_chunk(c):
                for half in range(2):
                    sqrt_var(2 * c + 1 + half, half * HALF, HALF)
                    save_x1(c, half)

            def until_last_word(c):
                end_of_chunk(c - 1)
                with act.Fori(0, G - 1) as g:
                    take_packs(c, g)
                stage_x1(c - 1, 0)
                stage_x1(c - 1, 1)
                project_chunk(c - 1)

            def sign_pair(c, r, b):
                at = parity(c) * CW
                m = r * BUFS + b
                act.wait_ge(c_ready, c * TP + m + 1)
                wait_apart(act, waits_apart)
                for k in range(2):
                    nc.scalar.activation(signs[:, b, k * CW:(k + 1) * CW], es_bc[:, bass.ds(at, CW)], ACT.Sign,
                                         bias=esed[:, bass.ds(2 * m + k, 1), 1]).then_inc(signs_ready, 1)

            with act.Fori(1, CH - 1) as c:
                until_last_word(c)
                take_packs(c, G - 1)
            until_last_word(CH - 1)
            act.wait_ge(es_landed, 16)
            for b in range(2):
                act.wait_ge(masks_used, LAST_TURN + 6 + b)
                sign_pair(0, 0, b)
            take_packs(CH - 1, G - 1)
            sqrt_var(2 * CH - 1, 0, HALF)
            save_x1(CH - 1, 0)
            stage_x1(CH - 1, 0)
            stage_x1(CH - 1, 1)
            sqrt_var(2 * CH, HALF, HALF)
            store_turned(CH - 1, 0)
            bring_exp()
            save_x1(CH - 1, 1)
            project_chunk(CH - 1, turned=1)
            sign_pair(0, 0, 2)
            act.wait_ge(shift_ready, 2)
            nc.scalar.activation(B_w, esed[:, :, 1], ACT.Exp, bias=shift[:, 0:1])
            nc.scalar.activation(Bp_w, esed[:, :, 1], ACT.Exp, bias=shift[:, 1:2], scale=SLOPE)
            nc.scalar.activation(al_w, w_lo, ACT.Exp)
            nc.scalar.activation(be_w, w_hi, ACT.Exp, scale=-1.0).then_inc(exp_done, 1)
            act.wait_ge(scale_ready, 2)

            def hi_c(jt):
                nc.scalar.activation(rows[:, jt, 0:DE], nodes_ext[:, jt, :], ACT.Copy,
                                     scale=B_w[:, bass.ds(jt, 1)]).then_inc(hi_c_ready, 1)

            def hi_d(jt, b):
                act.wait_ge(prod_d_ready, jt + 1)
                act.wait_ge(rows_c_ready, jt + 1)
                wait_apart(act, waits_apart)
                nc.scalar.activation(rows_d[:, jt, 0:DE], prod[:, 1, b, :], ACT.Copy).then_inc(hi_d_ready, 1)

            def scale_d(c):
                act.wait_ge(out_ready, 2 * c + 1)
                for i in range(CT):
                    act.wait_ge(c_taken, c * CT + i + 1)
                    wait_apart(act, waits_apart)
                    nc.scalar.activation(att[:, i, :], psum[:, i, 2 * DE:3 * DE], ACT.Copy,
                                         scale=be_w[:, bass.ds(c * CT + i, 1)]).then_inc(d_scaled, 1)

            def normalise(c, half):
                act.wait_ge(sums_ready, 2 * c + half + 1)
                for i in range(half * HALF, (half + 1) * HALF):
                    nc.scalar.activation(att[:, i, 0:D], att[:, i, 0:D], ACT.Copy,
                                         scale=rden[:, i:i + 1]).then_inc(norm_done, 1)

            def elu(c, half):
                tiles = slice(half * HALF, (half + 1) * HALF)
                act.wait_ge(att_ready, 2 * c + half + 1)
                wait_apart(act, waits_apart)
                nc.scalar.activation(exp_buf(c)[:, tiles, :], att[:, tiles, 0:D], ACT.Relu,
                                     scale=-1.0).then_inc(relu_done, 1)
                act.wait_ge(relu_done, 2 * c + half + 1)
                wait_apart(act, waits_apart)
                nc.scalar.activation(exp_buf(c)[:, tiles, :], exp_buf(c)[:, tiles, :], ACT.Exp,
                                     scale=-1.0).then_inc(elu_exp, 1)

            def sqrt1(c, half):
                sqrt_var(2 * CH + 2 * c + half + 1, half * HALF, HALF)

            def first_rows(m, r, b):
                last = isinstance(r, int)
                if not last or b + 3 < BUFS:
                    sign_pair(0, r + (b + 3) // BUFS, (b + 3) % BUFS)
                if not last or b + 2 < BUFS:
                    for n in range(2):
                        hi_c((m + 2) * 2 + n)
                if not last or b + 1 < BUFS:
                    for n in range(2):
                        hi_d((m + 1) * 2 + n, n)

            for jt in range(2):
                hi_c(jt)
            for jt in range(2):
                hi_d(jt, jt)
            for jt in range(2, 4):
                hi_c(jt)
            with act.Fori(0, TP // BUFS - 1) as r:
                for b in range(BUFS):
                    first_rows(r * BUFS + b, r, b)
            for b in range(BUFS):
                first_rows(TP - BUFS + b, TP // BUFS - 1, b)

            with act.Fori(1, CH) as c:
                act.wait_ge(es_landed, (c + 1) * 16)
                for m in range(3 * BUFS):
                    sign_pair(c, m // BUFS, m % BUFS)
                    if m == 3:
                        scale_d(c - 1)
                    for at, piece in ((5, normalise), (7, elu), (11, sqrt1)):
                        if m == at:
                            piece(c - 1, 0)
                            piece(c - 1, 1)
                with act.Fori(3, TP // BUFS) as r:
                    for b in range(BUFS):
                        sign_pair(c, r, b)
            bring_exp()
            scale_d(CH - 1)
            for piece in (normalise, elu, sqrt1):
                piece(CH - 1, 0)
                piece(CH - 1, 1)

        @block.vector
        def _(dve):
            dve.sem_inc(c_ready, BUFS)
            dve.sem_inc(masks_ready, 1)
            dve.sem_inc(d_ready, 1)
            dve.sem_inc(out_ready, 1)
            consts = Steps(dve, vec_consts)
            consts.did(nc.vector.memset(zeros[:], 0.0))
            consts.did(nc.vector.memset(ones[:], 1.0))
            consts.did(nc.vector.memset(a0_sb[:, 1:2], 1.0))
            consts.did(nc.vector.memset(big[:], 0.0))
            consts.did(nc.vector.memset(nodes_ext[:, :, D], 1.0))
            for k in range(BITS):
                consts.did(nc.vector.memset(bit_w[:, k:k + 1], float(2 ** k)))
            consts.settle()
            dve.sem_inc(consts_ready, 1)

            with dve.Fori(0, Q) as q:
                dve.wait_ge(inp_stored, q + 3)
                nc.vector.tensor_reduce(bits_w[:, bass.ds(q * 4, 4)], nodes[:, bass.ds(q * 4, 4), :], AX.X, ALU.max,
                                        apply_absolute_value=True).then_inc(vec_pro, 1)
            pro = Steps(dve, vec_pro, Q)

            def spread_maxima(n):
                dve.wait_ge(big_turned, n)
                pro.did(nc.vector.tensor_reduce(big_t[:], psum[0:2, 5, 128:256], AX.X, ALU.max))
                pro.settle()
                nc.vector.tensor_scalar(big_d[:], ident[0:2, 0:2], big_t[:, 0:1], None, ALU.mult).then_inc(big_diag, 1)
                dve.wait_ge(big_everywhere, n)

            e_all = psum[:, 4, 0:2 * T].rearrange("p (t two) -> p t two", two=2)
            dve.wait_ge(e_ready, Q + 2)
            nc.vector.tensor_reduce(big[:, 0:1], e_all[:, :, 0], AX.X, ALU.max).then_inc(big_ready, 1)
            dve.wait_ge(consts_ready, 2)
            spread_maxima(1)
            nc.vector.tensor_scalar(shift[:, 0:1], psum[:, 6, 0:1], -1.0, SHIFT, ALU.mult, ALU.add).then_inc(shift_ready, 1)
            dve.wait_ge(exp_done, 1)
            pro.did(nc.vector.scalar_tensor_tensor(out=p_w, in0=e_all[:, :, 1], scalar=0.0, in1=p_w,
                                                   op0=ALU.not_equal, op1=ALU.mult))
            pro.settle()
            pro.did(nc.vector.scalar_tensor_tensor(out=bits_w, in0=bits_w, scalar=1.0, in1=p_w,
                                                   op0=ALU.max, op1=ALU.mult))
            pro.settle()
            pro.did(nc.vector.tensor_scalar(bits_w, bits_w, 2.0 ** -100, None, ALU.max))
            pro.settle()
            pro.did(nc.vector.tensor_scalar(mask_w.bitcast(I32), bits_w.bitcast(I32), EXP_BITS, None, ALU.bitwise_and))
            pro.settle()
            pro.did(nc.vector.tensor_scalar(inv_w.bitcast(I32), mask_w.bitcast(I32), -1.0, float(EXP_TOP),
                                            ALU.mult, ALU.add))
            pro.settle()
            pro.did(nc.vector.scalar_tensor_tensor(out=q_w, in0=inv_w, scalar=PART_TOP, in1=p_w,
                                                   op0=ALU.mult, op1=ALU.mult))
            pro.did(nc.vector.tensor_tensor(pow_w.rearrange("p (g k) -> p g k", k=BITS),
                                            inv_w.rearrange("p (g k) -> p g k", k=BITS),
                                            bit_w[:].rearrange("p (o k) -> p o k", o=1).to_broadcast([P, G, BITS]),
                                            ALU.mult))
            pro.settle()
            pro.did(nc.vector.tensor_copy(rows[:, :, D], q_w))
            pro.settle()
            nc.vector.tensor_tensor(rows[:, :, DE + D], q_w, rows[:, :, D], ALU.subtract).then_inc(scale_ready, 1)

            def make_mask(c, g, k):
                n = (c * G + g) * BITS + k
                jt = g * BITS + k
                adj_tile = adj_in[:, k, :]
                if isinstance(c, int):
                    dve.wait_ge(hi_ready, jt + 1)
                    nc.vector.scalar_tensor_tensor(out=rows[:, jt, DE:DE + D], in0=nodes[:, jt, :],
                                                   scalar=q_w[:, bass.ds(jt, 1)], in1=rows[:, jt, 0:D],
                                                   op0=ALU.mult, op1=ALU.subtract).then_inc(rows_ready, 1)
                    if isinstance(g, int) and g == 1 and k >= BITS - 2 * EARLY:
                        adj_tile = adj_early[:, k - (BITS - 2 * EARLY), :]
                mask = seam if k == 0 else adj_in[:, k - 1, 0:CW // 2].bitcast(BF16)
                if k % 2 == 0:
                    dve.wait_ge(adj_landed[k // 2], (c * G + g + 1) * 16)
                dve.wait_ge(masks_used, n + 1)
                dve.wait_ge(masks_ready, n + 1)
                nc.vector.tensor_scalar(mask, adj_tile, 0.0, mask_w[:, bass.ds(jt, 1)],
                                        ALU.is_gt, ALU.mult).then_inc(masks_ready, 1)
                nc.vector.tensor_scalar(pack_w[:, k % AHEAD, :], ident_b[:], pow_w[:, bass.ds(jt, 1)], None,
                                        ALU.mult).then_inc(pack_w_ready, 1)

            def ln_stats(steps, tile, at, tiles):
                steps.settle()
                wait_apart(dve, waits_apart)
                for i in range(at, at + tiles):
                    steps.did(nc.vector.bn_stats(stats[:, i, :], tile(i)))
                steps.settle()
                wait_apart(dve, waits_apart)
                for i in range(at, at + tiles):
                    steps.did(nc.vector.bn_aggr(mv[:, i, :], stats[:, i, :]))
                steps.settle()
                nc.vector.tensor_scalar(var[:, at:at + tiles], mv[:, at:at + tiles, 1], EPS, None,
                                        ALU.add).then_inc(var_ready, 1)

            def ln_root(steps, n, at, tiles):
                dve.wait_ge(std_ready, n)
                steps.did(nc.vector.reciprocal(rstd[:, at:at + tiles], std[:, at:at + tiles]))
                steps.settle()

            def ln_apply(tile, at, tiles):
                for i in range(at, at + tiles):
                    last = nc.vector.tensor_scalar(tile(i), tile(i), mv[:, i, 0:1], rstd[:, i:i + 1],
                                                   ALU.subtract, ALU.mult)
                return last

            def node(c):
                return lambda i: nodes[:, c * CT + i, :]

            def divide_weights(steps, c, _):
                dve.wait_ge(masks_used, (c + 1) * T + AHEAD)
                for b in range(3):
                    column = bank(acc_bank(c), b, 0, 3 * DE).rearrange("p (t e) -> p t e", e=DE)[:, :, D]
                    steps.did(nc.vector.tensor_scalar(den[:, 3 * b:3 * b + 3], column, TINY, None, ALU.max))
                steps.settle()
                steps.did(nc.vector.reciprocal(rden[:], den[:]))
                steps.settle()

            def add_x(steps, c, at):
                if isinstance(c, int):
                    dve.wait_ge(last_x_landed, 16)
                    x_tiles = nodes[:, T - CT:, :]
                else:
                    dve.wait_ge(x_landed, 16 * 3)
                    x_tiles = x_buf(c)
                for i in (at, at + 1):
                    steps.did(nc.vector.scalar_tensor_tensor(out=nodes[:, c * CT + i, :],
                                                             in0=bank(acc_bank(c), i // 3, (i % 3) * DE, D),
                                                             scalar=rden[:, i:i + 1], in1=x_tiles[:, i, :],
                                                             op0=ALU.mult, op1=ALU.add))

            def stats0(steps, c, half):
                ln_stats(steps, node(c), half * HALF, HALF)

            def apply0(steps, c, at):
                if at % HALF == 0:
                    ln_root(steps, 2 * c + at // HALF + 1, at, HALF)
                last = ln_apply(node(c), at, 2)
                if (at + 2) % HALF == 0:
                    last.then_inc(x1_ready, 1)

            def h_maxima(steps, c, half):
                dve.wait_ge(h_stored, c * QC + (half + 1) * QC // 2)
                nc.vector.tensor_reduce(h_top[:, bass.ds(2 * c + half, 1)],
                                        nodes[:, bass.ds(c * CT + half * HALF, HALF), :], AX.XY, ALU.max,
                                        apply_absolute_value=True).then_inc(h_topped, 1)

            END_STEPS = 3 + 1 + CT + 2 * (CT + 1)
            for g in range(2):
                for k in range(BITS):
                    make_mask(0, g, k)
            with dve.Fori(2, G) as g:
                for k in range(BITS):
                    make_mask(0, g, k)
            with dve.Fori(1, CH) as c:
                pieces = {3: (divide_weights, 0), 4: (add_x, 0), 5: (add_x, 2), 6: (add_x, 4), 7: (add_x, 6),
                          8: (stats0, 0), 9: (stats0, 1), 10: (apply0, 0), 11: (apply0, 2), 12: (apply0, 4),
                          13: (apply0, 6)}
                steps = Steps(dve, ln_steps, (c - 1) * END_STEPS)
                for k in range(BITS):
                    make_mask(c, 0, k)
                    if k in pieces:
                        piece, at = pieces[k]
                        piece(steps, c - 1, at)
                assert steps.n == END_STEPS
                if G > 2:
                    with dve.Fori(1, G - 1) as g:
                        for k in range(BITS):
                            make_mask(c, g, k)
                for k in range(BITS):
                    make_mask(c, G - 1, k)
                h_maxima(steps, c - 1, 0)
                h_maxima(steps, c - 1, 1)
            def make_marks(c, g, kk):
                word = c * G + g
                if kk == BITS // 2:
                    word, kk = (word + 1) & (CH * G - 1), 0
                for n in range(2):
                    bit = 2 * kk + n
                    by, way = (14 - bit, ALU.logical_shift_left) if bit <= 14 else (bit - 14, ALU.logical_shift_right)
                    last = nc.vector.tensor_scalar(marks[:, kk % 2, n * CW:(n + 1) * CW].bitcast(U16),
                                                   packed[:, word, :], by, ONE_BITS, way, ALU.bitwise_and)
                last.then_inc(marks_ready, 1)

            def make_pair(c, g, kk):
                m = (c * G + g) * (BITS // 2) + kk
                b, mb = kk % BUFS, kk % 2
                dve.wait_ge(marks_ready, m + 1)
                dve.wait_ge(signs_ready, 2 * m + 2)
                dve.wait_ge(pairs_used, m + 1)
                nc.vector.tensor_tensor(mask_c[:, b, :], signs[:, b, :], marks[:, mb, :], ALU.is_gt).then_inc(c_ready, 1)
                dve.wait_ge(d_ready, m + 1)
                make_marks(c, g, kk + 1)
                dve.wait_ge(c_ready, m + BUFS + 1)
                nc.vector.tensor_tensor(mask_d[:, b, :], mask_c[:, b, :], marks[:, mb, :],
                                        ALU.is_equal).then_inc(d_ready, 1)

            def lo_c(m):
                for n in range(2):
                    jt = m * 2 + n
                    dve.wait_ge(hi_c_ready, jt + 1)
                    nc.vector.scalar_tensor_tensor(out=rows[:, jt, DE:2 * DE], in0=nodes_ext[:, jt, :],
                                                   scalar=B_w[:, bass.ds(jt, 1)], in1=rows[:, jt, 0:DE],
                                                   op0=ALU.mult, op1=ALU.subtract).then_inc(rows_c_ready, 1)

            steps = Steps(dve, ln_steps, (CH - 1) * END_STEPS)
            for piece, at in ((divide_weights, 0), (add_x, 0), (add_x, 2), (stats0, 0), (add_x, 4), (apply0, 0),
                              (apply0, 2), (add_x, 6), (stats0, 1), (apply0, 4), (apply0, 6)):
                piece(steps, CH - 1, at)
            make_marks(0, 0, 0)
            make_pair(0, 0, 0)
            h_maxima(steps, CH - 1, 0)
            make_pair(0, 0, 1)
            h_maxima(steps, CH - 1, 1)

            mid = Steps(dve, vec_mid)
            mid.did(nc.vector.tensor_reduce(big[:, 0:1], esed[:, :, 1], AX.X, ALU.max))
            dve.wait_ge(h_topped, 2 * CH)
            nc.vector.tensor_reduce(big[:, 1:2], h_top[:], AX.X, ALU.max).then_inc(big_ready, 1)
            pro.base, pro.n = pro.base + pro.n, 0
            spread_maxima(2)
            mid.did(nc.vector.tensor_scalar(shift[:, 0:1], psum[:, 6, 0:1], -1.0, None, ALU.mult))
            mid.did(nc.vector.tensor_scalar(shift[:, 1:2], psum[:, 6, 0:1], -SLOPE, None, ALU.mult))
            mid.settle()
            mid.did(nc.vector.tensor_scalar(mask_w, esed[:, :, 0], shift[:, 0:1], 1.0 - SLOPE, ALU.subtract, ALU.mult))
            mid.settle()
            mid.did(nc.vector.tensor_scalar(w_lo, mask_w, 0.0, None, ALU.min))
            nc.vector.tensor_scalar(w_hi, mask_w, 0.0, None, ALU.max).then_inc(shift_ready, 1)
            mid.did(nc.vector.tensor_scalar(shift[:, 2:3], psum[:, 6, 1:2], 1.0, None, ALU.max))
            mid.settle()
            mid.did(nc.vector.tensor_scalar(shift[:, 2:3].bitcast(I32), shift[:, 2:3].bitcast(I32), EXP_BITS, None,
                                            ALU.bitwise_and))
            mid.settle()
            mid.did(nc.vector.tensor_scalar(shift[:, 2:3].bitcast(I32), shift[:, 2:3].bitcast(I32), -1.0,
                                            float(EXP_TOP), ALU.mult, ALU.add))
            mid.settle()
            dve.wait_ge(exp_done, 2)
            mid.did(nc.vector.tensor_scalar(B_w, B_w, shift[:, 2:3], PART_TOP, ALU.mult, ALU.mult))
            nc.vector.tensor_scalar(Bp_w, Bp_w, shift[:, 2:3], PART_TOP, ALU.mult, ALU.mult).then_inc(scale_ready, 1)

            def take_sums(steps, c, half):
                if half == 0:
                    dve.wait_ge(pairs_used, (c + 1) * TP + BUFS)
                    wait_apart(dve, waits_apart)
                for i in range(half * HALF, (half + 1) * HALF, 2):
                    parts = psum[:, i:i + 2, 0:2 * DE].rearrange("p t (n e) -> p t e n", e=DE)
                    steps.did(nc.vector.tensor_reduce(c_weights[:, i:i + 2], parts[:, :, D, :], AX.X, ALU.add))
                    nc.vector.tensor_reduce(exp_buf(c)[:, i:i + 2, :], parts[:, :, 0:D, :], AX.X,
                                            ALU.add).then_inc(c_taken, 2)

            def weights(steps, c, half):
                tiles = slice(half * HALF, (half + 1) * HALF)
                dve.wait_ge(d_scaled, (c + 1) * CT + (half + 1) * HALF)
                steps.settle()
                steps.did(nc.vector.tensor_tensor(c_weights[:, tiles], c_weights[:, tiles],
                                                  al_w[:, bass.ds(c * CT + half * HALF, HALF)], ALU.mult))
                steps.settle()
                steps.did(nc.vector.tensor_tensor(c_weights[:, tiles], c_weights[:, tiles], att[:, tiles, D], ALU.add))
                steps.settle()
                steps.did(nc.vector.tensor_scalar(lone[:, tiles], c_weights[:, tiles], 0.0, None, ALU.is_le))
                steps.did(nc.vector.tensor_scalar(den[:, tiles], c_weights[:, tiles], TINY, None, ALU.max))
                steps.settle()
                steps.did(nc.vector.reciprocal(rden[:, tiles], den[:, tiles]))

            def add_c(steps, c, half):
                dve.wait_ge(c_taken, c * CT + (half + 1) * HALF)
                for i in range(half * HALF, (half + 1) * HALF):
                    last = nc.vector.scalar_tensor_tensor(out=att[:, i, 0:D], in0=exp_buf(c)[:, i, :],
                                                          scalar=al_w[:, bass.ds(c * CT + i, 1)], in1=att[:, i, 0:D],
                                                          op0=ALU.mult, op1=ALU.add)
                last.then_inc(sums_ready, 1)

            def add_mean(steps, c, half):
                dve.wait_ge(hmean_ready, 1)
                for i in range(half * HALF, (half + 1) * HALF):
                    dve.wait_ge(norm_done, c * CT + i + 1)
                    last = nc.vector.scalar_tensor_tensor(out=att[:, i, 0:D], in0=hmean, scalar=lone[:, i:i + 1],
                                                          in1=att[:, i, 0:D], op0=ALU.mult, op1=ALU.add)
                last.then_inc(att_ready, 1)

            def x1_tile(c):
                return lambda i: x1_buf(c)[:, i, :]

            def add_elu(steps, c, half):
                tiles = slice(half * HALF, (half + 1) * HALF)
                dve.wait_ge(elu_exp, 2 * c + half + 1)
                dve.wait_ge(att_ready, 2 * c + half + 1)
                steps.did(nc.vector.scalar_tensor_tensor(out=exp_buf(c)[:, tiles, :], in0=att[:, tiles, 0:D], scalar=0.0,
                                                         in1=exp_buf(c)[:, tiles, :], op0=ALU.max, op1=ALU.add))
                steps.settle()
                dve.wait_ge(x1_landed, (c + 1) * 16)
                steps.did(nc.vector.scalar_tensor_tensor(out=x1_buf(c)[:, tiles, :], in0=exp_buf(c)[:, tiles, :],
                                                         scalar=-1.0, in1=x1_buf(c)[:, tiles, :],
                                                         op0=ALU.add, op1=ALU.add))

            def stats1(steps, c, half):
                ln_stats(steps, x1_tile(c), half * HALF, HALF)

            def finish(steps, c, half):
                ln_root(steps, 2 * CH + 2 * c + half + 1, half * HALF, HALF)
                ln_apply(x1_tile(c), half * HALF, HALF).then_inc(out_ready, 1)

            OUT_STEPS = 2 * (HALF // 2 + 5 + 2 + 2 * HALF + 1)
            lo_c(0)
            lo_c(1)
            for kk in range(2, BITS // 2):
                lo_c(kk)
                make_pair(0, 0, kk)
            with dve.Fori(1, G) as g:
                for kk in range(BITS // 2):
                    lo_c(g * (BITS // 2) + kk)
                    make_pair(0, g, kk)
            with dve.Fori(1, CH) as c:
                steps = Steps(dve, out1_steps, (c - 1) * OUT_STEPS)
                pieces = {2: [(take_sums, 0), (take_sums, 1), (weights, 0), (weights, 1)], 3: [(add_c, 0)],
                          4: [(add_c, 1)], 7: [(add_elu, 0)], 8: [(add_elu, 1)], 9: [(stats1, 0)],
                          10: [(stats1, 1)], 12: [(finish, 0)], 13: [(finish, 1)]}
                for m in range(BITS):
                    make_pair(c, m // (BITS // 2), m % (BITS // 2))
                    for piece, half in pieces.get(m, []):
                        piece(steps, c - 1, half)
                assert steps.n == OUT_STEPS
                with dve.Fori(2, G) as g:
                    for kk in range(BITS // 2):
                        make_pair(c, g, kk)
            steps = Steps(dve, out1_steps, (CH - 1) * OUT_STEPS)
            for piece, half in ((take_sums, 0), (take_sums, 1), (weights, 0), (add_c, 0), (weights, 1), (add_c, 1),
                                (add_mean, 0), (add_mean, 1), (add_elu, 0), (stats1, 0), (add_elu, 1), (stats1, 1),
                                (finish, 0), (finish, 1)):
                piece(steps, CH - 1, half)

        @block.gpsimd
        def _(pool):
            own = Steps(pool, pool_steps)
            own.did(nc.gpsimd.memset(ident[:], 0.0))
            own.settle()
            own.did(nc.gpsimd.affine_select(out=ident[:], in_=ident[:], compare_op=ALU.not_equal, fill=1.0,
                                            base=0, pattern=[[-1, P]], channel_multiplier=1))
            own.settle()
            nc.gpsimd.tensor_copy(ident_b[:], ident[:]).then_inc(consts_ready, 1)

            nc.gpsimd.memset(hsum[:], 0.0).then_inc(hsum_steps, 1)
            with pool.Fori(0, CH) as c:
                for i in range(CT):
                    if i % 2 == 0:
                        pool.wait_ge(h_stored, c * QC + i // 2 + 1)
                    pool.wait_ge(hsum_steps, c * CT + i + 1)
                    wait_apart(pool, waits_apart)
                    nc.gpsimd.tensor_tensor(hsum[:], hsum[:], nodes[:, c * CT + i, :], ALU.add).then_inc(hsum_steps, 1)

            def product_d(jt, b):
                nc.gpsimd.tensor_tensor(prod[:, 1, b, :], nodes_ext[:, jt, :],
                                        Bp_w[:, bass.ds(jt, 1)].to_broadcast([P, DE]), ALU.mult).then_inc(prod_d_ready, 1)

            def lo_d(jt, b):
                pool.wait_ge(prod_d_ready, jt + 1)
                pool.wait_ge(hi_d_ready, jt + 1)
                wait_apart(pool, waits_apart)
                nc.gpsimd.tensor_tensor(rows_d[:, jt, DE:2 * DE], prod[:, 1, b, :], rows_d[:, jt, 0:DE],
                                        ALU.subtract).then_inc(rows1_ready, 1)
                pool.wait_ge(rows1_ready, jt + 1)
                wait_apart(pool, waits_apart)

            pool.wait_ge(hsum_steps, T + 1)
            pool.wait_ge(scale_ready, 2)
            product_d(0, 0)
            with pool.Fori(0, T // 2 - 1) as r:
                for b in range(2):
                    product_d(r * 2 + b + 1, 1 - b)
                    lo_d(r * 2 + b, b)
            product_d(T - 1, 1)
            lo_d(T - 2, 0)
            lo_d(T - 1, 1)

            pool.wait_ge(es_saved, 16 * (CH + 1))
            nc.gpsimd.partition_all_reduce(hmean, hsum[:], P, bass.bass_isa.ReduceOp.add).then_inc(mean_steps, 1)
            pool.wait_ge(mean_steps, 1)
            nc.gpsimd.tensor_scalar(hmean, hmean, 1.0 / N, 1.0, ALU.mult, ALU.mult).then_inc(hmean_ready, 1)

            pool.wait_ge(hmean_ready, 1)
            with pool.Fori(0, CH - 1) as c:
                for i in range(CT):
                    pool.wait_ge(norm_done, c * CT + i + 1)
                    nc.gpsimd.tensor_tensor(prod[:, 0, i % 2, 0:D], hmean, lone[:, i:i + 1].to_broadcast([P, D]),
                                            ALU.mult).then_inc(mean_steps, 1)
                    pool.wait_ge(mean_steps, c * CT + i + 2)
                    last = nc.gpsimd.tensor_tensor(att[:, i, 0:D], att[:, i, 0:D], prod[:, 0, i % 2, 0:D], ALU.add)
                    if i % HALF == HALF - 1:
                        last.then_inc(att_ready, 1)


def kernel(x, adj, L0_gnn_W, L0_gnn_b, L0_gnn_a, L1_gnn_W, L1_gnn_a):
    import numpy as np
    import concourse.bacc as bacc
    from concourse.bass_utils import run_bass_kernel_spmd

    x, adj, W1 = np.asarray(x), np.asarray(adj), np.asarray(L1_gnn_W)
    N = x.shape[0]
    blocks = adj.reshape(N // CW, CW, N // (2 * P), 2, P).transpose(0, 2, 4, 3, 1)
    arrays = {
        "x": x, "xT": x.T, "adj_blocks": blocks.reshape(-1, P, 2, CW),
        "W0": np.asarray(L0_gnn_W), "b0": np.asarray(L0_gnn_b), "a0": np.asarray(L0_gnn_a),
        "W1": W1, "W1T": W1.T, "a1": np.asarray(L1_gnn_a).reshape(2, D).T,
    }
    arrays = {name: np.ascontiguousarray(a) for name, a in arrays.items()}

    nc = bacc.Bacc("TRN2", target_bir_lowering=False, num_devices=1)
    aps = [nc.dram_tensor(name, a.shape, mybir.dt.from_np(a.dtype), kind="ExternalInput").ap()
           for name, a in arrays.items()]
    es_dram = nc.dram_tensor("es_by_node", (N,), F32, kind="Internal").ap()
    x1_dram = nc.dram_tensor("x1", (N, D), F32, kind="Internal").ap()
    out = nc.dram_tensor("out", (N, D), F32, kind="ExternalOutput").ap()
    gat_kernel(nc, *aps, es_dram, x1_dram, out)
    return run_bass_kernel_spmd(nc, [arrays], core_ids=[0]).results[0]["out"]
```
